# Optimizing a Trainium2 kernel written in Bass

```python
import numpy as np
import jax
import jax.numpy as jnp

def _softmax(x, axis=-1):
    return jax.nn.softmax(x, axis=axis)

def _gelu(x):
    return jax.nn.gelu(x, approximate=True)

def _silu(x):
    return jax.nn.silu(x)

def _sigmoid(x):
    return jax.nn.sigmoid(x)

def _layernorm(x, axis=-1, eps=1e-05):
    m = jnp.mean(x, axis=axis, keepdims=True)
    v = jnp.var(x, axis=axis, keepdims=True)
    return (x - m) / jnp.sqrt(v + eps)

def _scatter_add(tgt, idx, src, axis=0):
    return tgt.at[idx].add(src)

def _segment_sum(src, seg, n):
    return jax.ops.segment_sum(src, seg, n)
kernel_name = 'mk_gnn_resnorm_d1_gnn_r8_773186'

def setup_inputs(seed: int=0):
    np.random.seed(seed)
    _w = jnp.asarray

    def _rec_inputs():
        import jax
        import jax.numpy as jnp
        _gk = jax.random.key(seed)
        x = -0.000202 + 1 * jax.random.normal(jax.random.fold_in(_gk, 1), (6250, 128), jnp.float32)
        _s = jax.random.randint(jax.random.fold_in(_gk, 2), (50000,), 0, 6250, jnp.int32)
        _d = jax.random.randint(jax.random.fold_in(_gk, 3), (50000,), 0, 6250, jnp.int32)
        _loop = jnp.arange(6250, dtype=jnp.int32)
        src = jnp.concatenate([_s, _d, _loop])
        dst = jnp.concatenate([_d, _s, _loop])
        _o = jnp.argsort(dst, stable=True)
        src = src[_o]
        dst = dst[_o]
        edge_type_8 = jax.random.randint(jax.random.fold_in(_gk, 12), (106250,), 0, 8, jnp.int32)
        return (x, src, dst, edge_type_8)
    x, src, dst, edge_type_8 = _rec_inputs()

    def _L0_gnn_setup():
        import jax, jax.numpy as jnp
        import numpy as np
        N = 6250
        E = 200000
        D = 128
        R = 8
        L = 3

        def _rgcn_layer(x, src, dst, edge_type, W, W_root, b):
            n = x.shape[0]
            out = x @ W_root + b
            x_src = x[src]
            for r in range(R):
                mask = (edge_type == r).astype(x.dtype)
                agg = jax.ops.segment_sum(x_src * mask[:, None], dst, num_segments=n)
                cnt = jax.ops.segment_sum(mask, dst, num_segments=n)
                mean = agg / jnp.maximum(cnt, 1.0)[:, None]
                out = out + mean @ W[r]
            return out
        key = jax.random.key(seed)
        ks = jax.random.split(key, 6)
        x = jax.random.normal(ks[0], (N, D), dtype=jnp.float32)
        edge_index = jax.random.randint(ks[1], (2, E), 0, N)
        edge_type = jax.random.randint(ks[2], (E,), 0, R)
        scale = 1.0 / np.sqrt(D)
        Ws = jax.random.normal(ks[3], (L, R, D, D), dtype=jnp.float32) * scale
        W_roots = jax.random.normal(ks[4], (L, D, D), dtype=jnp.float32) * scale
        bs = jnp.zeros((L, D), dtype=jnp.float32)
        return {'x': x, 'edge_index': edge_index, 'edge_type': edge_type, 'Ws': Ws, 'W_roots': W_roots, 'bs': bs}
    _L0_gnn_all = _L0_gnn_setup()
    _L0_gnn_in = {k: v for k, v in _L0_gnn_all.items() if k in ('Ws', 'W_roots', 'bs')}
    del _L0_gnn_all
    return {'x': x, 'src': src, 'dst': dst, 'edge_type_8': edge_type_8, 'L0_gnn_Ws': _L0_gnn_in['Ws'], 'L0_gnn_W_roots': _L0_gnn_in['W_roots'], 'L0_gnn_bs': _L0_gnn_in['bs']}

def reference(x, src, dst, edge_type_8, L0_gnn_Ws, L0_gnn_W_roots, L0_gnn_bs):
    import jax
    import jax.numpy as jnp

    def _L0_gnn_ref(x, edge_index, edge_type, Ws, W_roots, bs):
        import jax, jax.numpy as jnp
        import numpy as np
        N = 6250
        E = 200000
        D = 128
        R = 8
        L = 3

        def _rgcn_layer(x, src, dst, edge_type, W, W_root, b):
            n = x.shape[0]
            out = x @ W_root + b
            x_src = x[src]
            for r in range(R):
                mask = (edge_type == r).astype(x.dtype)
                agg = jax.ops.segment_sum(x_src * mask[:, None], dst, num_segments=n)
                cnt = jax.ops.segment_sum(mask, dst, num_segments=n)
                mean = agg / jnp.maximum(cnt, 1.0)[:, None]
                out = out + mean @ W[r]
            return out
        src, dst = (edge_index[0], edge_index[1])
        h = x
        for i in range(L):
            h = _rgcn_layer(h, src, dst, edge_type, Ws[i], W_roots[i], bs[i])
            if i < L - 1:
                h = jax.nn.relu(h)
        return h
    edge_index = jnp.stack([src, dst])
    x = _layernorm(x + _L0_gnn_ref(x, edge_index, edge_type_8, L0_gnn_Ws, L0_gnn_W_roots, L0_gnn_bs), axis=-1)
    return x

_drawn_inputs = setup_inputs


def setup_inputs(seed=0):
    import zlib

    import numpy as np

    out = dict(_drawn_inputs(seed))
    spreads = {'L0_gnn_bs': (0.0, 0.1)}
    factors = {}
    for name, (base, spread) in spreads.items():
        noise = np.random.default_rng([zlib.crc32(name.encode()), seed]).standard_normal(out[name].shape)
        drawn = base * np.exp(spread * noise) if base else spread * noise
        out[name] = jnp.asarray(drawn.astype(out[name].dtype))
    for name, factor in factors.items():
        out[name] = (out[name] * factor).astype(out[name].dtype)
    return out
```

```python
from contextlib import ExitStack

import concourse.bass as bass
from concourse import mybir

F32 = mybir.dt.float32
BF16 = mybir.dt.bfloat16
I32 = mybir.dt.int32
ALU = mybir.AluOpType
ACT = mybir.ActivationFunctionType
AX = mybir.AxisListType

N = 6250
E = 106250
D = 128
R = 8
L = 3
P = 128
EPS = 1e-5

RAW = -(-E // (P * P))
FULL = E // (P * P)
TAIL = (E - FULL * P * P) // P
REST = E - FULL * P * P - TAIL * P
CH = 32
GT = 4
G = CH // GT
NI = -(-E // (P * CH))
NT = NI * CH
WIN = 16
KEYS = R * WIN
BLK = 512
NB = -(-N // BLK)
NS = -(-N // P)
TB = BLK // P
NTAIL = N - (NS - 1) * P
NPAD = N + WIN


def rgcn(nc, x, src, dst, typ, Ws, Wr, bs, out, table):
    with ExitStack() as ctx:
        def sb(name, shape, dt):
            return ctx.enter_context(nc.sbuf_tensor(name, shape, dt))

        def sem(name):
            return ctx.enter_context(nc.semaphore(name))

        def pair(name):
            return [sem(f"{name}{i}") for i in range(2)]

        ident = sb("ident", [P, P], F32)
        ident_bf = sb("ident_bf", [P, P], BF16)
        iota_i = sb("iota_i", [P, P], I32)
        iota = sb("iota", [P, P], F32)
        eps = sb("eps", [P, 1], F32)
        raw_src = sb("raw_src", [P, RAW, P], I32)
        raw_dst = sb("raw_dst", [P, RAW, P], I32)
        raw_typ = sb("raw_typ", [P, RAW, P], I32)
        low = sb("low", [P, RAW], F32)
        high = sb("high", [P, RAW], F32)
        src_t = sb("src_t", [P, RAW * P], I32)
        rel_t = sb("rel_t", [P, RAW * P], F32)
        typ_t = sb("typ_t", [P, RAW * P], F32)
        rel_k = sb("rel_k", [P, NT], F32)
        key = sb("key", [P, NT], F32)
        m_a = sb("m_a", [P, NT], F32)
        m_b = sb("m_b", [P, NT], F32)
        weight = sb("weight", [P, NT], F32)
        base_f = sb("base_f", [1, RAW * P], F32)
        span_f = sb("span_f", [1, RAW * P], F32)
        base_0 = sb("base_0", [1, NT], I32)
        base_k = sb("base_k", [1, NT], I32)
        span_i = sb("span_i", [1, 2], I32)
        passes = sb("passes", [1, 1], I32)
        idx = sb("idx", [P, G, GT], I32)
        ring = sb("ring", [P, G, GT, D], F32)
        onehot = sb("onehot", [P, 2, GT, KEYS], F32)
        oh_typ = sb("oh_typ", [P, CH, R], BF16)
        oh_dst = sb("oh_dst", [P, CH, WIN], BF16)
        picked = sb("picked", [P, CH, WIN], F32)
        picked_sum = sb("picked_sum", [P, CH], F32)
        wide = sb("wide", [P, 2, BLK], F32)
        count = sb("count", [R, NPAD], F32)
        h_t = sb("h_t", [D, NB * BLK], F32)
        out_t = sb("out_t", [D, NS * P], F32)
        rows = sb("rows", [P, NB * TB, D], F32)
        f_src, f_dst, f_typ = (rows[:, n * RAW:(n + 1) * RAW, :] for n in range(3))
        x_rows = out_t[:, :].rearrange("p (t d) -> p t d", d=D)
        x_again = h_t[:, 0:NS * P].rearrange("p (t d) -> p t d", d=D)
        w_rel = sb("w_rel", [D, R, D], F32)
        w_root = sb("w_root", [D, D], F32)
        bias = sb("bias", [D, 1], F32)
        stats = sb("stats", [P, NS, 6], F32)
        moments = sb("moments", [P, NS, 2], F32)
        std = sb("std", [P, NS], F32)
        rstd = sb("rstd", [P, NS], F32)

        ps_a = [ctx.enter_context(nc.psum_tensor(f"ps_a{i}", [P, BLK], F32)) for i in range(2)]
        ps_o = [ctx.enter_context(nc.psum_tensor(f"ps_o{i}", [P, BLK], F32)) for i in range(2)]
        ps_r = [ctx.enter_context(nc.psum_tensor(f"ps_r{i}", [P, BLK], F32)) for i in range(2)]

        edges_in = sem("edges_in")
        x_in = sem("x_in")
        w_in = sem("w_in")
        table_in = sem("table_in")
        out_in = sem("out_in")
        const_step = sem("const_step")
        const_ready = sem("const_ready")
        raw_cleared = sem("raw_cleared")
        dve_step = sem("dve_step")
        act_step = sem("act_step")
        low_ready = sem("low_ready")
        rel_ready = sem("rel_ready")
        index_ready = sem("index_ready")
        passes_ready = [sem(f"passes_ready_{e}") for e in ("pe", "act", "pool")]
        count_ready = sem("count_ready")
        window_ready = sem("window_ready")
        h_ready = sem("h_ready")
        w_ready = sem("w_ready")
        w_used = sem("w_used")
        root_added = sem("root_added")
        sums_ready = sem("sums_ready")
        block_full = pair("block_full")
        block_free = pair("block_free")
        rows_full = sem("rows_full")
        table_ready = sem("table_ready")
        idx_full = [sem(f"idx_full{q}") for q in range(G)]
        gathered = [sem(f"gathered{q}") for q in range(G)]
        picks_full = sem("picks_full")
        oh_full = pair("oh_full")
        oh_free = pair("oh_free")
        a_full = pair("a_full")
        a_free = pair("a_free")
        wide_full = pair("wide_full")
        wide_free = pair("wide_free")
        o_full = pair("o_full")
        o_free = pair("o_free")
        r_full_act = pair("r_full_act")
        r_full_dve = pair("r_full_dve")
        r_free = pair("r_free")
        h_free = sem("h_free")
        var_ready = sem("var_ready")
        std_ready = sem("std_ready")
        out_full = sem("out_full")

        def take(eng, credit):
            eng.wait_ge(credit, 1)
            eng.sem_inc(credit, -1)

        def load_value(eng, ap, lo, hi, why):
            _, v = nc.values_load_multi_w_load_instructions(
                ap, engines=[eng.engine], min_val=lo, max_val=hi, skip_runtime_bounds_check_because=why)
            return v

        def load_passes(eng):
            return load_value(eng, passes[0:1, 0:1], 1, N // WIN + 1,
                              "a span of node numbers over the window")[0]

        def load_bases(eng, start, n):
            return load_value(eng, base_k[0:1, bass.ds(start, n)], 0, N, "the chip clamps them to N")

        def block_cols(n):
            return min(BLK, N - n * BLK)

        def tile_rows(n):
            return min(P, N - n * P)

        def blocks_of(n):
            return range(n * TB, min((n + 1) * TB, NS))

        block = ctx.enter_context(nc.Block())

        @block.sync
        def _(sp):
            cut = FULL * P * P
            for raw, flat in ((raw_dst, dst), (raw_src, src), (raw_typ, typ)):
                sp.dma_start(raw[:, 0:FULL, :], flat[0:cut].rearrange("(b p e) -> p b e", p=P, e=P))\
                  .then_inc(edges_in, 16)
            sp.wait_ge(raw_cleared, 3)
            for raw, flat in ((raw_dst, dst), (raw_src, src), (raw_typ, typ)):
                sp.dma_start(raw[0:TAIL, FULL, :],
                             flat[cut:cut + TAIL * P].rearrange("(p e) -> p e", e=P))\
                  .then_inc(edges_in, 16)
                sp.dma_start(raw[TAIL:TAIL + 1, FULL, 0:REST],
                             flat[E - REST:E].rearrange("(p e) -> p e", p=1)).then_inc(edges_in, 16)
            sp.dma_start(raw_dst[TAIL:TAIL + 1, FULL, REST:P],
                         dst[E - (P - REST):E].rearrange("(p e) -> p e", p=1))\
              .then_inc(edges_in, 16)
            whole = (NS - 1) * P
            sp.dma_start(x_rows[:, 0:NS - 1, :], x[0:whole, :].rearrange("(t p) d -> p t d", p=P))\
              .then_inc(x_in, 16)
            sp.dma_start(x_rows[0:NTAIL, NS - 1, :], x[whole:N, :]).then_inc(x_in, 16)
            sp.dma_start(table, x).then_inc(table_in, 16)
            sp.wait_ge(table_in, 16)
            sp.sem_inc(table_ready, 1)

            def load_weights(layer, landed):
                sp.dma_start(w_rel[:, :, :], Ws[bass.ds(layer, 1), :, :, :].rearrange("l r k d -> k (l r) d"))\
                  .then_inc(w_in, 16)
                sp.dma_start(w_root[:, :], Wr[bass.ds(layer, 1), :, :].rearrange("l k d -> (l k) d"))\
                  .then_inc(w_in, 16)
                sp.dma_start(bias[:, :], bs[bass.ds(layer, 1), :].rearrange("l d -> d l"))\
                  .then_inc(w_in, 16)
                sp.wait_ge(w_in, landed)
                sp.sem_inc(w_ready, 1)

            load_weights(0, 48)
            with sp.Fori(1, L) as layer:
                take(sp, w_used)
                load_weights(layer, layer * 48 + 48)
                for n in range(NB):
                    take(sp, rows_full)
                    lo, cols = n * BLK, block_cols(n)
                    if cols == BLK:
                        sp.dma_start(table[lo:lo + BLK, :].rearrange("(t p) d -> p t d", p=P),
                                     rows[:, n * TB:(n + 1) * TB, :]).then_inc(table_in, 16)
                    else:
                        sp.dma_start(table[lo:N, :], rows[0:cols, n * TB, :]).then_inc(table_in, 16)
                sp.wait_ge(table_in, layer * (16 * NB) + 16)
                sp.sem_inc(table_ready, 1)
            take(sp, h_free)
            sp.dma_start(x_again[:, 0:NS - 1, :], x[0:whole, :].rearrange("(t p) d -> p t d", p=P))\
              .then_inc(x_in, 16)
            sp.dma_start(x_again[0:NTAIL, NS - 1, :], x[whole:N, :]).then_inc(x_in, 16)
            for n in range(NB):
                take(sp, out_full)
                lo, cols = n * BLK, block_cols(n)
                if cols == BLK:
                    sp.dma_start(out[lo:lo + BLK, :].rearrange("(t p) d -> p t d", p=P),
                                 rows[:, n * TB:(n + 1) * TB, :]).then_inc(out_in, 16)
                else:
                    sp.dma_start(out[lo:N, :], rows[0:cols, n * TB, :]).then_inc(out_in, 16)
            sp.wait_ge(out_in, 16 * NB)

        @block.gpsimd
        def _(pool):
            nc.gpsimd.memset(raw_typ[:, FULL, :], 15).then_inc(raw_cleared, 1)
            nc.gpsimd.memset(raw_dst[:, FULL, :], 0).then_inc(raw_cleared, 1)
            nc.gpsimd.memset(raw_src[:, FULL, :], 0).then_inc(raw_cleared, 1)
            nc.gpsimd.memset(ident[:, :], 0.0).then_inc(const_step, 1)
            nc.gpsimd.memset(eps[:, :], EPS).then_inc(const_ready, 1)
            nc.gpsimd.iota(iota_i[:, :], pattern=[[1, P]], base=0, channel_multiplier=0).then_inc(const_ready, 1)
            pool.wait_ge(const_step, 1)
            nc.gpsimd.affine_select(out=ident[:, :], in_=ident[:, :], compare_op=ALU.not_equal, fill=1.0,
                                    base=0, pattern=[[-1, P]], channel_multiplier=1).then_inc(const_ready, 1)

            def gather_pass():
                with pool.Fori(0, NI):
                    for q in range(G):
                        take(pool, idx_full[q])
                        for t in range(GT):
                            nc.gpsimd.indirect_dma_start(
                                out=ring[:, q, t, :], out_offset=None, in_=table,
                                in_offset=bass.IndirectOffsetOnAxis(ap=idx[:, q, t:t + 1], axis=0))\
                              .then_inc(gathered[q], 16)

            take(pool, passes_ready[2])
            count_of = load_passes(pool)
            with pool.Fori(0, L):
                take(pool, table_ready)
                with pool.Fori(0, count_of):
                    gather_pass()

        @block.vector
        def _(dve):
            def done(ins):
                ins.then_inc(dve_step, 1)
                dve.wait_ge(dve_step, 1)
                dve.sem_inc(dve_step, -1)

            dve.wait_ge(const_ready, 3)
            nc.vector.tensor_copy(iota[:, :], iota_i[:, :])
            done(nc.vector.tensor_copy(ident_bf[:, :], ident[:, :]))
            nc.vector.memset(count[:, :], 0.0)
            done(nc.vector.memset(weight[:, :], 0.0))
            dve.wait_ge(edges_in, 16 * 10)
            done(nc.vector.tensor_copy(f_dst[:, :, :], raw_dst[:, :, :]))
            done(nc.vector.tensor_reduce(low[:, :], f_dst[:, :, :], AX.X, ALU.min))
            done(nc.vector.tensor_reduce(high[:, :], f_dst[:, :, :], AX.X, ALU.max))
            done(nc.vector.tensor_tensor(high[:, :], high[:, :], low[:, :], ALU.subtract))
            dve.sem_inc(low_ready, 1)
            nc.vector.tensor_copy(f_src[:, :, :], raw_src[:, :, :])
            nc.vector.tensor_copy(f_typ[:, :, :], raw_typ[:, :, :])
            done(nc.vector.tensor_tensor(f_dst[:, :, :], f_dst[:, :, :],
                                         low[:, :].unsqueeze(2).broadcast_to([P, RAW, P]), ALU.subtract))
            dve.sem_inc(rel_ready, 1)
            for n, row in enumerate((base_f, span_f)):
                for b in range(2):
                    lo, hi = b * BLK, min((b + 1) * BLK, RAW * P)
                    take(dve, r_full_dve[b])
                    nc.vector.tensor_copy(row[0:1, lo:hi], ps_r[b][0:1, 0:hi - lo]).then_inc(r_free[b], 1)
            done(nc.vector.memset(span_i[:, :], 0))
            nc.vector.tensor_copy(base_0[:, :], base_f[:, 0:NT])
            done(nc.vector.tensor_reduce(span_i[0:1, 0:1], span_f[0:1, :], AX.X, ALU.max))
            done(nc.vector.tensor_scalar(span_i[0:1, 1:2], span_i[0:1, 0:1], WIN.bit_length() - 1, None,
                                         ALU.arith_shift_right))
            done(nc.vector.tensor_scalar(passes[:, :], span_i[0:1, 1:2], 1.0, None, ALU.add))
            for s in passes_ready:
                dve.sem_inc(s, 1)
            count_of = load_passes(dve)
            take(dve, index_ready)
            for q in range(G):
                nc.vector.tensor_copy(idx[:, q, :], src_t[:, q * GT:(q + 1) * GT]).then_inc(idx_full[q], 1)
            done(nc.vector.tensor_copy(src_t[:, NT:NT + CH], src_t[:, 0:CH]))

            def first_windows():
                nc.vector.tensor_copy(base_k[:, :], base_0[:, :])
                done(nc.vector.tensor_copy(rel_k[:, :], rel_t[:, 0:NT]))

            def next_windows():
                nc.vector.tensor_scalar(base_k[:, :], base_k[:, :], float(WIN), float(N), ALU.add, ALU.min)
                done(nc.vector.tensor_scalar(rel_k[:, :], rel_k[:, :], float(WIN), None, ALU.subtract))

            def pick(col):
                nc.vector.tensor_tensor(
                    oh_typ[:, :, :], typ_t[:, bass.ds(col, CH)].unsqueeze(2).broadcast_to([P, CH, R]),
                    iota[:, 0:R].unsqueeze(1).broadcast_to([P, CH, R]), ALU.is_equal)
                done(nc.vector.tensor_tensor(
                    oh_dst[:, :, :], rel_k[:, bass.ds(col, CH)].unsqueeze(2).broadcast_to([P, CH, WIN]),
                    iota[:, 0:WIN].unsqueeze(1).broadcast_to([P, CH, WIN]), ALU.is_equal))
                dve.sem_inc(picks_full, 1)

            first_windows()
            with dve.Fori(0, count_of):
                with dve.Fori(0, NI) as it:
                    pick(it * CH)
                    take(dve, r_full_dve[0])
                    for q in range(G):
                        start = load_bases(dve, it * CH + q * GT, GT)
                        for t in range(GT):
                            at = (q * GT + t) * WIN
                            here = count[:, bass.ds(start[t], WIN)]
                            done(nc.vector.tensor_tensor(here, here, ps_r[0][0:R, at:at + WIN], ALU.add))
                    dve.sem_inc(r_free[0], 1)
                next_windows()
            done(nc.vector.tensor_scalar(count[:, :], count[:, :], 1.0, None, ALU.max))
            done(nc.vector.reciprocal(count[:, :], count[:, :]))
            dve.sem_inc(count_ready, 1)

            first_windows()
            with dve.Fori(0, count_of):
                dve.sem_inc(window_ready, 1)
                with dve.Fori(0, NI) as it:
                    pick(it * CH)
                    take(dve, r_full_dve[0])
                    dve.sem_inc(wide_free[(G - 1) % 2], 1)
                    done(nc.vector.tensor_tensor(
                        picked[:, :, :], oh_dst[:, :, :],
                        ps_r[0][:, :].rearrange("p (c w) -> p c w", w=WIN), ALU.mult))
                    dve.sem_inc(r_free[0], 1)
                    done(nc.vector.tensor_reduce(picked_sum[:, :], picked[:, :, :], AX.X, ALU.add))
                    here = weight[:, bass.ds(it * CH, CH)]
                    done(nc.vector.tensor_tensor(here, here, picked_sum[:, :], ALU.add))
                next_windows()

            def keys():
                nc.vector.tensor_scalar(m_a[:, :], rel_k[:, :], 0.0, None, ALU.is_ge)
                done(nc.vector.tensor_scalar(m_b[:, :], rel_k[:, :], float(WIN), None, ALU.is_lt))
                done(nc.vector.tensor_tensor(m_a[:, :], m_a[:, :], m_b[:, :], ALU.mult))
                done(nc.vector.tensor_scalar(m_b[:, :], typ_t[:, 0:NT], float(WIN), 1.0, ALU.mult, ALU.add))
                done(nc.vector.tensor_tensor(m_b[:, :], m_b[:, :], rel_k[:, :], ALU.add))
                done(nc.vector.tensor_tensor(m_b[:, :], m_b[:, :], m_a[:, :], ALU.mult))
                done(nc.vector.tensor_scalar(key[:, :], m_b[:, :], 1.0, None, ALU.subtract))

            def weigh(it, q):
                b = q % 2
                for t in range(GT):
                    col = it * CH + (q * GT + t)
                    ins = nc.vector.tensor_scalar(
                        onehot[:, b, t, :], iota[:, :], key[:, bass.ds(col, 1)],
                        weight[:, bass.ds(col, 1)], ALU.is_equal, ALU.mult)
                ins.then_inc(oh_full[b], 1)

            def refill(it, q):
                take(dve, oh_free[q % 2])
                nc.vector.tensor_copy(idx[:, q, :], src_t[:, bass.ds((it + 1) * CH + q * GT, GT)])\
                  .then_inc(idx_full[q], 1)

            def add_out(it, q):
                b = q % 2
                start = load_bases(dve, it * CH + q * GT, GT)
                take(dve, o_full[b])
                dve.sem_inc(wide_free[b], 1)
                for t in range(GT):
                    here = out_t[:, bass.ds(start[t], WIN)]
                    done(nc.vector.tensor_tensor(here, here, ps_o[b][:, t * WIN:(t + 1) * WIN], ALU.add))
                dve.sem_inc(o_free[b], 1)

            def layer_sums():
                first_windows()
                take(dve, root_added)
                with dve.Fori(0, count_of):
                    keys()
                    with dve.Fori(0, NI) as it:
                        weigh(it, 0)
                        weigh(it, 1)
                        for q in range(G):
                            refill(it, q)
                            if q + 2 < G:
                                weigh(it, q + 2)
                            add_out(it, q)
                    next_windows()
                dve.sem_inc(sums_ready, 1)

            with dve.Fori(0, L - 1):
                layer_sums()
                for n in range(NB):
                    b = n % 2
                    take(dve, r_full_dve[b])
                    dve.sem_inc(block_free[b], 1)
                    part = tile_rows(n * TB)
                    done(nc.vector.tensor_copy(
                        rows[0:part, n * TB:n * TB + len(blocks_of(n)), :],
                        ps_r[b][0:part, 0:len(blocks_of(n)) * D].rearrange("p (t d) -> p t d", d=D)))
                    dve.sem_inc(r_free[b], 1)
                    dve.sem_inc(rows_full, 1)
            layer_sums()

            dve.wait_ge(x_in, 64)
            for n in range(NB):
                b = n % 2
                take(dve, r_full_dve[b])
                part, tiles = tile_rows(n * TB), len(blocks_of(n))
                done(nc.vector.tensor_tensor(
                    rows[0:part, n * TB:n * TB + tiles, :], x_again[0:part, n * TB:n * TB + tiles, :],
                    ps_r[b][0:part, 0:tiles * D].rearrange("p (t d) -> p t d", d=D), ALU.add))
                dve.sem_inc(r_free[b], 1)
                for s in blocks_of(n):
                    ins = nc.vector.bn_stats(stats[0:part, s, :], rows[0:part, s, :])
                done(ins)
                for s in blocks_of(n):
                    ins = nc.vector.bn_aggr(moments[0:part, s, :], stats[0:part, s, :])
                done(ins)
            dve.sem_inc(var_ready, 1)
            take(dve, std_ready)
            nc.vector.reciprocal(rstd[:, 0:NS - 1], std[:, 0:NS - 1])
            done(nc.vector.reciprocal(rstd[0:NTAIL, NS - 1:NS], std[0:NTAIL, NS - 1:NS]))
            for n in range(NB):
                for s in blocks_of(n):
                    part = tile_rows(s)
                    ins = nc.vector.tensor_scalar(rows[0:part, s, :], rows[0:part, s, :],
                                                  moments[0:part, s, 0:1], rstd[0:part, s:s + 1],
                                                  ALU.subtract, ALU.mult)
                ins.then_inc(out_full, 1)

        @block.scalar
        def _(act):
            for b in range(2):
                act.sem_inc(a_free[b], 1)
            for n, to in enumerate((src_t, rel_t, typ_t)):
                for b in range(2):
                    lo, hi = b * BLK, min((b + 1) * BLK, RAW * P)
                    take(act, r_full_act[b])
                    nc.scalar.copy(to[:, lo:hi], ps_r[b][:, 0:hi - lo]).then_inc(act_step, 1)
                    act.wait_ge(act_step, 1)
                    act.sem_inc(act_step, -1)
                    act.sem_inc(r_free[b], 1)
            act.sem_inc(index_ready, 1)
            for n in range(NB):
                b, cols = n % 2, block_cols(n)
                take(act, r_full_act[b])
                nc.scalar.copy(h_t[:, n * BLK:n * BLK + cols], ps_r[b][:, 0:cols]).then_inc(act_step, 1)
                act.wait_ge(act_step, 1)
                act.sem_inc(act_step, -1)
                act.sem_inc(r_free[b], 1)
            act.sem_inc(h_ready, 1)
            take(act, passes_ready[1])
            count_of = load_passes(act)
            with act.Fori(0, count_of):
                with act.Fori(0, NI):
                    for q in range(G):
                        b = q % 2
                        take(act, a_full[b])
                        take(act, wide_free[b])
                        nc.scalar.copy(wide[0:R, b, :], ps_a[b][0:R, :]).then_inc(act_step, 1)
                        act.wait_ge(act_step, 1)
                        act.sem_inc(act_step, -1)
                        act.sem_inc(a_free[b], 1)
                        act.sem_inc(wide_full[b], 1)

            def root_and_sums(last=False):
                for n in range(NB):
                    b, cols = n % 2, block_cols(n)
                    take(act, r_full_act[b])
                    nc.scalar.activation(out_t[:, n * BLK:n * BLK + cols], ps_r[b][:, 0:cols], ACT.Identity,
                                         bias=bias[:, 0:1]).then_inc(act_step, 1)
                    act.wait_ge(act_step, 1)
                    act.sem_inc(act_step, -1)
                    act.sem_inc(r_free[b], 1)
                act.sem_inc(root_added, 1)
                if last:
                    act.sem_inc(h_free, 1)
                with act.Fori(0, count_of):
                    with act.Fori(0, NI):
                        for q in range(G):
                            b = q % 2
                            take(act, a_full[b])
                            act.sem_inc(oh_free[b], 1)
                            take(act, wide_free[b])
                            nc.scalar.copy(
                                wide[:, b, :].rearrange("p (r t w) -> p t r w", r=R, t=GT),
                                ps_a[b][:, :].rearrange("p (t r w) -> p t r w", r=R, t=GT))\
                              .then_inc(act_step, 1)
                            act.wait_ge(act_step, 1)
                            act.sem_inc(act_step, -1)
                            act.sem_inc(a_free[b], 1)
                            act.sem_inc(wide_full[b], 1)

            nc.scalar.activation(out_t[:, N:NPAD], iota[:, 0:WIN], ACT.Copy, scale=0.0).then_inc(act_step, 1)
            act.wait_ge(act_step, 1)
            act.sem_inc(act_step, -1)
            with act.Fori(0, L - 1):
                root_and_sums()
                take(act, sums_ready)
                for n in range(NB):
                    b, cols = n % 2, block_cols(n)
                    take(act, block_free[b])
                    nc.scalar.activation(h_t[:, n * BLK:n * BLK + cols], out_t[:, n * BLK:n * BLK + cols],
                                         ACT.Relu).then_inc(block_full[b], 1)
            root_and_sums(last=True)
            take(act, sums_ready)
            act.sem_inc(block_full[0], 1)
            take(act, var_ready)
            nc.scalar.activation(std[:, 0:NS - 1], moments[:, 0:NS - 1, 1], ACT.Sqrt, bias=eps[:, 0:1])
            nc.scalar.activation(std[0:NTAIL, NS - 1:NS], moments[0:NTAIL, NS - 1, 1:2], ACT.Sqrt,
                                 bias=eps[0:NTAIL, 0:1]).then_inc(act_step, 1)
            act.wait_ge(act_step, 1)
            act.sem_inc(std_ready, 1)

        @block.tensor
        def _(pe):
            for b in range(2):
                pe.sem_inc(r_free[b], 1)
                pe.sem_inc(wide_free[b], 1)
                pe.sem_inc(o_free[b], 1)
                pe.sem_inc(block_free[b], 1)
            pe.wait_ge(const_ready, 3)
            take(pe, low_ready)
            for cols in (low, high):
                for b in range(2):
                    take(pe, r_free[b])
                    for n in range(b * TB, min((b + 1) * TB, RAW)):
                        ins = nc.tensor.matmul(ps_r[b][0:1, (n - b * TB) * P:(n - b * TB + 1) * P],
                                               cols[:, n:n + 1], ident[:, :], start=True, stop=True)
                    ins.then_inc(r_full_dve[b], 1)
            take(pe, rel_ready)
            for raw in (f_src, f_dst, f_typ):
                for b in range(2):
                    take(pe, r_free[b])
                    for n in range(b * TB, min((b + 1) * TB, RAW)):
                        ins = nc.tensor.transpose(ps_r[b][:, (n - b * TB) * P:(n - b * TB + 1) * P],
                                                  raw[:, n, :], ident[:, :])
                    ins.then_inc(r_full_act[b], 1)
            pe.wait_ge(x_in, 32)
            for n in range(NB):
                b = n % 2
                take(pe, r_free[b])
                for s in blocks_of(n):
                    part, at = tile_rows(s), (s - n * TB) * P
                    ins = nc.tensor.transpose(ps_r[b][:, at:at + part], x_rows[0:part, s, :],
                                              ident[0:part, 0:part])
                ins.then_inc(r_full_act[b], 1)
            take(pe, passes_ready[0])
            count_of = load_passes(pe)

            with pe.Fori(0, count_of):
                with pe.Fori(0, NI):
                    take(pe, picks_full)
                    take(pe, r_free[0])
                    for c in range(CH):
                        ins = nc.tensor.matmul(ps_r[0][0:R, c * WIN:(c + 1) * WIN], oh_typ[:, c, :],
                                               oh_dst[:, c, :], start=True, stop=True)
                    ins.then_inc(r_full_dve[0], 1)

            take(pe, count_ready)
            with pe.Fori(0, count_of):
                take(pe, window_ready)
                with pe.Fori(0, NI) as it:
                    def turn(q):
                        b = q % 2
                        take(pe, a_free[b])
                        for t in range(GT):
                            ins = nc.tensor.matmul(ps_a[b][0:R, t * P:(t + 1) * P],
                                                   oh_typ[:, q * GT + t, :], ident_bf[:, :],
                                                   start=True, stop=True)
                        ins.then_inc(a_full[b], 1)

                    def look_up(q):
                        b = q % 2
                        start = load_bases(pe, it * CH + q * GT, GT)
                        take(pe, wide_full[b])
                        for t in range(GT):
                            at = (q * GT + t) * WIN
                            ins = nc.tensor.matmul(ps_r[0][:, at:at + WIN], wide[0:R, b, t * P:(t + 1) * P],
                                                   count[:, bass.ds(start[t], WIN)], start=True, stop=True)
                        ins.then_inc(wide_free[b] if q + 1 < G else r_full_dve[0], 1)

                    take(pe, picks_full)
                    take(pe, r_free[0])
                    turn(0)
                    for q in range(G):
                        if q + 1 < G:
                            turn(q + 1)
                        look_up(q)

            done_of = pe.alloc_register("gathers_done")
            pe.reg_mov(done_of, 0)

            def sum_edges(q, target):
                b = q % 2
                take(pe, oh_full[b])
                take(pe, a_free[b])
                pe.wait_ge(gathered[q], target)
                for t in range(GT):
                    ins = nc.tensor.matmul(ps_a[b][:, t * KEYS:(t + 1) * KEYS], ring[:, q, t, :],
                                           onehot[:, b, t, :], start=True, stop=True)
                ins.then_inc(a_full[b], 1)

            def apply_types(q):
                b = q % 2
                take(pe, wide_full[b])
                take(pe, o_free[b])
                for r in range(R):
                    ins = nc.tensor.matmul(ps_o[b][:, 0:GT * WIN], w_rel[:, r, :],
                                           wide[:, b, r * GT * WIN:(r + 1) * GT * WIN],
                                           start=(r == 0), stop=(r == R - 1))
                ins.then_inc(o_full[b], 1)

            def root_and_sums():
                take(pe, w_ready)
                for n in range(NB):
                    b, cols = n % 2, block_cols(n)
                    take(pe, r_free[b])
                    nc.tensor.matmul(ps_r[b][:, 0:cols], w_root[:, :], h_t[:, n * BLK:n * BLK + cols],
                                     start=True, stop=True).then_inc(r_full_act[b], 1)
                with pe.Fori(0, count_of):
                    with pe.Fori(0, NI):
                        pe.reg_add(done_of, done_of, GT * 16)
                        target = pe.snap(done_of)
                        sum_edges(0, target)
                        for q in range(G):
                            if q + 1 < G:
                                sum_edges(q + 1, target)
                            apply_types(q)

            take(pe, h_ready)
            with pe.Fori(0, L - 1):
                root_and_sums()
                for n in range(NB):
                    b = n % 2
                    take(pe, block_full[b])
                    if n == 0:
                        pe.sem_inc(w_used, 1)
                    take(pe, r_free[b])
                    for s in blocks_of(n):
                        part, at = tile_rows(s), (s - n * TB) * D
                        ins = nc.tensor.transpose(ps_r[b][0:part, at:at + D],
                                                  h_t[:, s * P:s * P + part], ident[:, :])
                    ins.then_inc(r_full_dve[b], 1)
            root_and_sums()
            take(pe, block_full[0])
            for n in range(NB):
                b = n % 2
                take(pe, r_free[b])
                for s in blocks_of(n):
                    part, at = tile_rows(s), (s - n * TB) * D
                    ins = nc.tensor.transpose(ps_r[b][0:part, at:at + D],
                                              out_t[:, s * P:s * P + part], ident[:, :])
                ins.then_inc(r_full_dve[b], 1)


_INS = ["x", "src", "dst", "edge_type_8", "L0_gnn_Ws", "L0_gnn_W_roots", "L0_gnn_bs"]


def kernel(**inputs):
    import numpy as _np
    import concourse.bacc as _bacc
    from concourse import mybir as _mybir
    from concourse.bass_utils import run_bass_kernel_spmd as _run

    nc = _bacc.Bacc("TRN2", target_bir_lowering=False, num_devices=1)
    arrays, args = {}, []
    for name in _INS:
        a = _np.ascontiguousarray(inputs[name])
        arrays[f"in_{name}"] = a
        args.append(nc.dram_tensor(f"in_{name}", a.shape, _mybir.dt.from_np(a.dtype), kind="ExternalInput").ap())
    out = nc.dram_tensor("out_rows", (N, D), F32, kind="ExternalOutput").ap()
    table = nc.dram_tensor("node_table", (N, D), F32, kind="Internal").ap()
    rgcn(nc, *args, out, table)
    r = _run(nc, [arrays], core_ids=[0])
    return r.results[0]["out_rows"]
```

```python
from contextlib import ExitStack

import concourse.bass as bass
from concourse import mybir

F32 = mybir.dt.float32
BF16 = mybir.dt.bfloat16
I32 = mybir.dt.int32
ALU = mybir.AluOpType
ACT = mybir.ActivationFunctionType
AX = mybir.AxisListType

N = 6250
E = 106250
D = 128
R = 8
L = 3
P = 128
EPS = 1e-5

RAW = -(-E // (P * P))
FULL = E // (P * P)
TAIL = (E - FULL * P * P) // P
REST = E - FULL * P * P - TAIL * P
CH = 32
GT = 4
G = CH // GT
PAIR = 2 * GT
NI = -(-E // (P * CH))
NT = NI * CH
WIN = 16
KEYS = R * WIN
BUCKETS = -(-N // WIN)
BWIN = 8
PARTS = 3
NO_TYPE = 2000
BLK = 512
NB = -(-N // BLK)
NS = -(-N // P)
TB = BLK // P
NTAIL = N - (NS - 1) * P
NPAD = N + WIN
BPAD = BUCKETS + BWIN


def rgcn(nc, x, src, dst, typ, Ws, Wr, bs, out, table):
    with ExitStack() as ctx:
        def sb(name, shape, dt):
            return ctx.enter_context(nc.sbuf_tensor(name, shape, dt))

        def sem(name):
            return ctx.enter_context(nc.semaphore(name))

        def pair(name):
            return [sem(f"{name}{i}") for i in range(2)]

        ident = sb("ident", [P, P], F32)
        ident_bf = sb("ident_bf", [P, P], BF16)
        zeros = sb("zeros", [P, BLK], BF16)
        iota_i = sb("iota_i", [P, P], I32)
        iota = sb("iota", [P, P], F32)
        iota_bf = sb("iota_bf", [P, P], BF16)
        eps = sb("eps", [P, 1], F32)
        raw_src = sb("raw_src", [P, RAW, P], I32)
        raw_dst = sb("raw_dst", [P, RAW, P], I32)
        raw_typ = sb("raw_typ", [P, RAW, P], I32)
        bkt_i = sb("bkt_i", [P, RAW, P], I32)
        node_i = sb("node_i", [P, RAW, P], I32)
        low = sb("low", [P, RAW], F32)
        high = sb("high", [P, RAW], F32)
        low_bkt = sb("low_bkt", [P, RAW], F32)
        src_t = sb("src_t", [P, RAW * P], I32)
        rel_t = sb("rel_t", [P, RAW * P], F32)
        typ_t = sb("typ_t", [P, RAW * P], F32)
        cell_t = sb("cell_t", [P, RAW * P], BF16)
        brel_t = sb("brel_t", [P, RAW * P], F32)
        rel_k = sb("rel_k", [P, NT], F32)
        brel_k = sb("brel_k", [P, NT + CH], F32)
        key = sb("key", [P, NT], F32)
        m_a = sb("m_a", [P, NT], F32)
        m_b = sb("m_b", [P, NT], F32)
        weight = sb("weight", [P, NT + CH], F32)
        base_f = sb("base_f", [1, RAW * P], F32)
        span_f = sb("span_f", [1, RAW * P], F32)
        base_0 = sb("base_0", [1, NT + CH], I32)
        base_k = sb("base_k", [1, NT + CH], I32)
        bucket_0 = sb("bucket_0", [1, NT + CH], I32)
        bucket_k = sb("bucket_k", [1, NT + CH], I32)
        span_i = sb("span_i", [1, 4], I32)
        passes = sb("passes", [1, 2], I32)
        idx = sb("idx", [P, G, GT], I32)
        ring = sb("ring", [P, G, GT, D], F32)
        onehot = sb("onehot", [P, 2, GT, KEYS], F32)
        oh_cell = sb("oh_cell", [P, 2, GT, P], BF16)
        oh_cell_t = sb("oh_cell_t", [P, 2, GT * P], BF16)
        oh_bkt = sb("oh_bkt", [P, CH, BWIN], BF16)
        picked = sb("picked", [P, CH, 2, PARTS], F32)
        sums = sb("sums", [D, 2, R, PAIR, WIN], F32)
        inverse = sb("inverse", [P, BPAD], F32)
        inv_rest = sb("inv_rest", [P, BPAD], F32)
        inv_parts = sb("inv_parts", [P, BPAD, PARTS], BF16)
        h_t = sb("h_t", [D, NB * BLK], F32)
        out_t = sb("out_t", [D, NS * P], F32)
        rows = sb("rows", [P, NB * TB, D], F32)
        f_src, f_dst, f_typ, f_bkt, f_cell = (rows[:, n * RAW:(n + 1) * RAW, :] for n in range(5))
        x_rows = out_t[:, :].rearrange("p (t d) -> p t d", d=D)
        x_again = h_t[:, 0:NS * P].rearrange("p (t d) -> p t d", d=D)
        w_rel = sb("w_rel", [D, R, D], F32)
        w_root = sb("w_root", [D, D], F32)
        bias = sb("bias", [D, 1], F32)
        stats = sb("stats", [P, NS, 6], F32)
        moments = sb("moments", [P, NB * TB, 2], F32)
        std = sb("std", [P, NB * TB], F32)
        rstd = sb("rstd", [P, NB * TB], F32)
        shift = sb("shift", [P, NB * TB], F32)

        ps_a = [ctx.enter_context(nc.psum_tensor(f"ps_a{i}", [P, BLK], F32)) for i in range(2)]
        ps_o = [ctx.enter_context(nc.psum_tensor(f"ps_o{i}", [P, BLK], F32)) for i in range(2)]
        ps_r = [ctx.enter_context(nc.psum_tensor(f"ps_r{i}", [P, BLK], F32)) for i in range(2)]
        ps_c = ctx.enter_context(nc.psum_tensor("ps_c", [P, BLK], F32))
        ps_w = ctx.enter_context(nc.psum_tensor("ps_w", [P, BLK], F32))

        dst_in = sem("dst_in")
        typ_in = sem("typ_in")
        src_in = sem("src_in")
        x_in = sem("x_in")
        w_in = sem("w_in")
        table_in = sem("table_in")
        out_in = sem("out_in")
        const_step = sem("const_step")
        const_ready = sem("const_ready")
        raw_cleared = sem("raw_cleared")
        dve_step = sem("dve_step")
        act_step = sem("act_step")
        low_ready = sem("low_ready")
        bkt_ready = sem("bkt_ready")
        src_ready = sem("src_ready")
        rel_ready = sem("rel_ready")
        index_ready = sem("index_ready")
        bkt_rows_ready = sem("bkt_rows_ready")
        passes_ready = [sem(f"passes_ready_{e}") for e in ("pe", "act", "pool")]
        bkt_full = sem("bkt_full")
        bkt_free = sem("bkt_free")
        windows_free = sem("windows_free")
        cell_full = pair("cell_full")
        cell_free = pair("cell_free")
        turned_full = pair("turned_full")
        turned_free = pair("turned_free")
        count_full = sem("count_full")
        parts_ready = sem("parts_ready")
        windows_full = sem("windows_full")
        weights_full = sem("weights_full")
        weights_free = sem("weights_free")
        h_ready = sem("h_ready")
        w_ready = sem("w_ready")
        w_used = sem("w_used")
        root_added = sem("root_added")
        sums_ready = [sem(f"sums_ready_{e}") for e in ("pe", "act")]
        rows_full = pair("rows_full")
        table_ready = sem("table_ready")
        idx_full = [sem(f"idx_full{q}") for q in range(G)]
        gathered = [sem(f"gathered{q}") for q in range(G)]
        oh_full = pair("oh_full")
        oh_free = pair("oh_free")
        a_full = pair("a_full")
        a_free = pair("a_free")
        sums_full = pair("sums_full")
        sums_free = pair("sums_free")
        added = sem("added")
        o_full = pair("o_full")
        o_free = pair("o_free")
        r_full_act = pair("r_full_act")
        r_full_dve = pair("r_full_dve")
        r_free = pair("r_free")
        h_free = sem("h_free")
        residual_in = sem("residual_in")
        stats_in = sem("stats_in")
        var_ready = sem("var_ready")
        std_ready = sem("std_ready")
        rstd_ready = sem("rstd_ready")
        shift_ready = sem("shift_ready")
        out_full = sem("out_full")

        def take(eng, credit):
            eng.wait_ge(credit, 1)
            eng.sem_inc(credit, -1)

        def load_value(eng, ap, lo, hi, why):
            _, v = nc.values_load_multi_w_load_instructions(
                ap, engines=[eng.engine], min_val=lo, max_val=hi, skip_runtime_bounds_check_because=why)
            return v

        def load_passes(eng):
            return load_value(eng, passes[0:1, 0:1], 1, BUCKETS + 1, "a span of nodes over the window")[0]

        def load_bases(eng, start, n):
            return load_value(eng, base_k[0:1, bass.ds(start, n)], 0, N, "the chip clamps them to N")

        def load_buckets(eng, start, n):
            return load_value(eng, bucket_k[0:1, bass.ds(start, n)], 0, BUCKETS,
                              "the chip clamps them to the number of buckets")

        def block_cols(n):
            return min(BLK, N - n * BLK)

        def tile_rows(n):
            return min(P, N - n * P)

        def blocks_of(n):
            return range(n * TB, min((n + 1) * TB, NS))

        block = ctx.enter_context(nc.Block())

        @block.sync
        def _(sp):
            cut = FULL * P * P
            sp.wait_ge(raw_cleared, 3)
            for raw, flat, landed in ((raw_dst, dst, dst_in), (raw_typ, typ, typ_in), (raw_src, src, src_in)):
                sp.dma_start(raw[:, 0:FULL, :], flat[0:cut].rearrange("(b p e) -> p b e", p=P, e=P))\
                  .then_inc(landed, 16)
                sp.dma_start(raw[0:TAIL, FULL, :],
                             flat[cut:cut + TAIL * P].rearrange("(p e) -> p e", e=P))\
                  .then_inc(landed, 16)
                sp.dma_start(raw[TAIL:TAIL + 1, FULL, 0:REST],
                             flat[E - REST:E].rearrange("(p e) -> p e", p=1)).then_inc(landed, 16)
                if raw is raw_dst:
                    sp.dma_start(raw[TAIL:TAIL + 1, FULL, REST:P],
                                 flat[E - (P - REST):E].rearrange("(p e) -> p e", p=1)).then_inc(landed, 16)
            sp.dma_start(table, x).then_inc(table_in, 16)
            whole = (NS - 1) * P
            sp.dma_start(x_rows[:, 0:NS - 1, :], x[0:whole, :].rearrange("(t p) d -> p t d", p=P))\
              .then_inc(x_in, 16)
            sp.dma_start(x_rows[0:NTAIL, NS - 1, :], x[whole:N, :]).then_inc(x_in, 16)
            sp.wait_ge(table_in, 16)
            sp.sem_inc(table_ready, 1)

            def load_weights(layer, landed):
                sp.dma_start(w_rel[:, :, :], Ws[bass.ds(layer, 1), :, :, :].rearrange("l r k d -> k (l r) d"))\
                  .then_inc(w_in, 16)
                sp.dma_start(w_root[:, :], Wr[bass.ds(layer, 1), :, :].rearrange("l k d -> (l k) d"))\
                  .then_inc(w_in, 16)
                sp.dma_start(bias[:, :], bs[bass.ds(layer, 1), :].rearrange("l d -> d l"))\
                  .then_inc(w_in, 16)
                sp.wait_ge(w_in, landed)
                sp.sem_inc(w_ready, 1)

            load_weights(0, 48)
            with sp.Fori(1, L) as layer:
                take(sp, w_used)
                load_weights(layer, layer * 48 + 48)
                for n in range(NB):
                    take(sp, rows_full[n % 2])
                    lo, cols = n * BLK, block_cols(n)
                    if cols == BLK:
                        sp.dma_start(table[lo:lo + BLK, :].rearrange("(t p) d -> p t d", p=P),
                                     rows[:, n * TB:(n + 1) * TB, :]).then_inc(table_in, 16)
                    else:
                        sp.dma_start(table[lo:N, :], rows[0:cols, n * TB, :]).then_inc(table_in, 16)
                sp.wait_ge(table_in, layer * (16 * NB) + 16)
                sp.sem_inc(table_ready, 1)
            take(sp, h_free)
            sp.dma_start(x_again[:, 0:NS - 1, :], x[0:whole, :].rearrange("(t p) d -> p t d", p=P))\
              .then_inc(x_in, 16)
            sp.dma_start(x_again[0:NTAIL, NS - 1, :], x[whole:N, :]).then_inc(x_in, 16)
            for n in range(NB):
                take(sp, out_full)
                lo, cols = n * BLK, block_cols(n)
                if cols == BLK:
                    sp.dma_start(out[lo:lo + BLK, :].rearrange("(t p) d -> p t d", p=P),
                                 rows[:, n * TB:(n + 1) * TB, :]).then_inc(out_in, 16)
                else:
                    sp.dma_start(out[lo:N, :], rows[0:cols, n * TB, :]).then_inc(out_in, 16)
            sp.wait_ge(out_in, 16 * NB)

        @block.gpsimd
        def _(pool):
            nc.gpsimd.memset(raw_typ[:, FULL, :], NO_TYPE).then_inc(raw_cleared, 1)
            nc.gpsimd.memset(raw_dst[:, FULL, :], 0).then_inc(raw_cleared, 1)
            nc.gpsimd.memset(raw_src[:, FULL, :], 0).then_inc(raw_cleared, 1)
            nc.gpsimd.memset(ident[:, :], 0.0).then_inc(const_step, 1)
            nc.gpsimd.memset(eps[:, :], EPS).then_inc(const_ready, 1)
            nc.gpsimd.iota(iota_i[:, :], pattern=[[1, P]], base=0, channel_multiplier=0).then_inc(const_ready, 1)
            pool.wait_ge(const_step, 1)
            nc.gpsimd.affine_select(out=ident[:, :], in_=ident[:, :], compare_op=ALU.not_equal, fill=1.0,
                                    base=0, pattern=[[-1, P]], channel_multiplier=1).then_inc(const_ready, 1)

            def gather_pass():
                with pool.Fori(0, NI):
                    for q in range(G):
                        take(pool, idx_full[q])
                        for t in range(GT):
                            nc.gpsimd.indirect_dma_start(
                                out=ring[:, q, t, :], out_offset=None, in_=table,
                                in_offset=bass.IndirectOffsetOnAxis(ap=idx[:, q, t:t + 1], axis=0))\
                              .then_inc(gathered[q], 16)

            take(pool, passes_ready[2])
            count_of = load_passes(pool)
            with pool.Fori(0, L):
                take(pool, table_ready)
                with pool.Fori(0, count_of):
                    gather_pass()

        @block.vector
        def _(dve):
            def done(ins):
                ins.then_inc(dve_step, 1)
                dve.wait_ge(dve_step, 1)
                dve.sem_inc(dve_step, -1)

            dve.wait_ge(dst_in, 16 * 4)
            nc.vector.tensor_scalar(bkt_i[:, :, :], raw_dst[:, :, :], WIN.bit_length() - 1, None,
                                    ALU.arith_shift_right)
            nc.vector.tensor_scalar(node_i[:, :, :], raw_dst[:, :, :], WIN - 1, None, ALU.bitwise_and)
            done(nc.vector.tensor_copy(f_dst[:, :, :], raw_dst[:, :, :]))
            nc.vector.tensor_reduce(low[:, :], f_dst[:, :, :], AX.X, ALU.min)
            nc.vector.tensor_reduce(high[:, :], f_dst[:, :, :], AX.X, ALU.max)
            done(nc.vector.tensor_reduce(low_bkt[:, :], bkt_i[:, :, :], AX.X, ALU.min))
            nc.vector.tensor_tensor(f_bkt[:, :, :], bkt_i[:, :, :],
                                    low_bkt[:, :].unsqueeze(2).broadcast_to([P, RAW, P]), ALU.subtract)
            done(nc.vector.tensor_tensor(high[:, :], high[:, :], low[:, :], ALU.subtract))
            dve.sem_inc(low_ready, 1)
            dve.wait_ge(typ_in, 16 * 3)
            done(nc.vector.scalar_tensor_tensor(f_cell[:, :, :], node_i[:, :, :], float(R), raw_typ[:, :, :],
                                                ALU.mult, ALU.add))
            dve.sem_inc(bkt_ready, 1)
            dve.wait_ge(src_in, 16 * 3)
            done(nc.vector.tensor_copy(f_src[:, :, :], raw_src[:, :, :]))
            dve.sem_inc(src_ready, 1)
            dve.wait_ge(const_ready, 3)
            nc.vector.tensor_copy(iota[:, :], iota_i[:, :])
            nc.vector.tensor_copy(iota_bf[:, :], iota_i[:, :])
            nc.vector.memset(zeros[:, :], 0.0)
            nc.vector.tensor_copy(ident_bf[:, :], ident[:, :])
            nc.vector.tensor_copy(f_typ[:, :, :], raw_typ[:, :, :])
            done(nc.vector.tensor_tensor(f_dst[:, :, :], f_dst[:, :, :],
                                         low[:, :].unsqueeze(2).broadcast_to([P, RAW, P]), ALU.subtract))
            dve.sem_inc(rel_ready, 1)
            for row in (base_f, span_f):
                for b in range(2):
                    lo, hi = b * BLK, min((b + 1) * BLK, RAW * P)
                    take(dve, r_full_dve[b])
                    done(nc.vector.tensor_copy(row[0:1, lo:hi], ps_r[b][0:1, 0:hi - lo]))
                    dve.sem_inc(r_free[b], 1)
            done(nc.vector.tensor_copy(base_0[:, :], base_f[:, 0:NT + CH]))
            nc.vector.tensor_scalar(bucket_0[:, :], base_0[:, :], WIN.bit_length() - 1, None,
                                    ALU.arith_shift_right)
            done(nc.vector.tensor_reduce(span_i[0:1, 0:1], span_f[0:1, :], AX.X, ALU.max))
            done(nc.vector.tensor_scalar(span_i[0:1, 1:2], span_i[0:1, 0:1], WIN.bit_length() - 1, None,
                                         ALU.arith_shift_right))
            done(nc.vector.tensor_scalar(passes[:, 0:1], span_i[0:1, 1:2], 1.0, None, ALU.add))
            done(nc.vector.tensor_scalar(span_i[0:1, 3:4], passes[0:1, 0:1], BWIN.bit_length() - 1, None,
                                         ALU.arith_shift_right))
            done(nc.vector.tensor_scalar(passes[:, 1:2], span_i[0:1, 3:4], 1.0, None, ALU.add))
            for s in passes_ready:
                dve.sem_inc(s, 1)
            count_of = load_passes(dve)
            counts_of = load_value(dve, passes[0:1, 1:2], 1, BUCKETS, "a span of buckets over 8")[0]

            def cells(start, q):
                b = q % 2
                take(dve, cell_free[b])
                nc.vector.tensor_tensor(
                    oh_cell[:, b, :, :],
                    cell_t[:, bass.ds(start + q * GT, GT)].unsqueeze(2).broadcast_to([P, GT, P]),
                    iota_bf[:, :].unsqueeze(1).broadcast_to([P, GT, P]), ALU.is_equal).then_inc(cell_full[b], 1)

            take(dve, bkt_rows_ready)
            nc.vector.tensor_copy(bucket_k[:, :], bucket_0[:, :])
            done(nc.vector.tensor_copy(brel_k[:, :], brel_t[:, 0:NT + CH]))
            with dve.Fori(0, counts_of):
                dve.sem_inc(windows_full, 1)
                with dve.Fori(0, NI) as it:
                    take(dve, bkt_free)
                    dve.sem_inc(cell_free[(G - 1) % 2], 1)
                    nc.vector.tensor_tensor(
                        oh_bkt[:, :, :], brel_k[:, bass.ds(it * CH, CH)].unsqueeze(2).broadcast_to([P, CH, BWIN]),
                        iota[:, 0:BWIN].unsqueeze(1).broadcast_to([P, CH, BWIN]), ALU.is_equal)\
                        .then_inc(bkt_full, 1)
                    for q in range(G):
                        cells(it * CH, q)
                take(dve, windows_free)
                nc.vector.tensor_scalar(bucket_k[:, :], bucket_k[:, :], float(BWIN), float(BUCKETS),
                                        ALU.add, ALU.min)
                done(nc.vector.tensor_scalar(brel_k[:, :], brel_k[:, :], float(BWIN), None, ALU.subtract))
            take(dve, bkt_free)
            dve.sem_inc(cell_free[(G - 1) % 2], 1)
            take(dve, count_full)
            done(nc.vector.tensor_scalar(inverse[:, :], ps_c[:, 0:BPAD], 1.0, None, ALU.max))
            done(nc.vector.reciprocal(inverse[:, :], inverse[:, :]))
            done(nc.vector.tensor_copy(inv_parts[:, :, 0], inverse[:, :]))
            done(nc.vector.tensor_tensor(inv_rest[:, :], inverse[:, :], inv_parts[:, :, 0], ALU.subtract))
            done(nc.vector.tensor_copy(inv_parts[:, :, 1], inv_rest[:, :]))
            done(nc.vector.tensor_tensor(inv_parts[:, :, 2], inv_rest[:, :], inv_parts[:, :, 1], ALU.subtract))
            dve.sem_inc(parts_ready, 1)

            take(dve, index_ready)
            done(nc.vector.tensor_copy(src_t[:, NT:NT + CH], src_t[:, 0:CH]))

            def first_windows():
                nc.vector.tensor_copy(base_k[:, :], base_0[:, :])
                nc.vector.tensor_copy(bucket_k[:, :], bucket_0[:, :])
                nc.vector.tensor_copy(brel_k[:, :], brel_t[:, 0:NT + CH])
                done(nc.vector.tensor_copy(rel_k[:, :], rel_t[:, 0:NT]))

            def next_windows():
                nc.vector.tensor_scalar(base_k[:, :], base_k[:, :], float(WIN), float(N), ALU.add, ALU.min)
                nc.vector.tensor_scalar(bucket_k[:, :], bucket_k[:, :], 1.0, float(BUCKETS), ALU.add, ALU.min)
                nc.vector.tensor_scalar(brel_k[:, :], brel_k[:, :], 1.0, None, ALU.subtract)
                done(nc.vector.tensor_scalar(rel_k[:, :], rel_k[:, :], float(WIN), None, ALU.subtract))

            def weights(start):
                take(dve, weights_full)
                dve.sem_inc(turned_free[(G - 1) % 2], 1)
                done(nc.vector.tensor_tensor(
                    oh_bkt[:, :, 0:2], brel_k[:, bass.ds(start, CH)].unsqueeze(2).broadcast_to([P, CH, 2]),
                    iota[:, 0:2].unsqueeze(1).broadcast_to([P, CH, 2]), ALU.is_equal))
                done(nc.vector.tensor_tensor(
                    picked[:, :, :, :], ps_w[:, 0:CH * 2 * PARTS].rearrange("p (c w k) -> p c w k", w=2, k=PARTS),
                    oh_bkt[:, :, 0:2].unsqueeze(3).broadcast_to([P, CH, 2, PARTS]), ALU.mult))
                dve.sem_inc(weights_free, 1)
                done(nc.vector.tensor_reduce(weight[:, bass.ds(start, CH)],
                                             picked[:, :, :, :].rearrange("p c w k -> p c (w k)"), AX.X, ALU.add))

            def keys():
                nc.vector.tensor_scalar(m_a[:, :], rel_k[:, :], 0.0, None, ALU.is_ge)
                done(nc.vector.tensor_scalar(m_b[:, :], rel_k[:, :], float(WIN), None, ALU.is_lt))
                done(nc.vector.tensor_tensor(m_a[:, :], m_a[:, :], m_b[:, :], ALU.mult))
                done(nc.vector.tensor_scalar(m_b[:, :], typ_t[:, 0:NT], float(WIN), 1.0, ALU.mult, ALU.add))
                done(nc.vector.tensor_tensor(m_b[:, :], m_b[:, :], rel_k[:, :], ALU.add))
                done(nc.vector.tensor_tensor(m_b[:, :], m_b[:, :], m_a[:, :], ALU.mult))
                done(nc.vector.tensor_scalar(key[:, :], m_b[:, :], 1.0, None, ALU.subtract))

            def weigh(it, q, t):
                b, col = q % 2, it * CH + (q * GT + t)
                ins = nc.vector.tensor_scalar(
                    onehot[:, b, t, :], iota[:, :], key[:, bass.ds(col, 1)],
                    weight[:, bass.ds(col, 1)], ALU.is_equal, ALU.mult)
                if t + 1 == GT:
                    ins.then_inc(oh_full[b], 1)

            def refill(it, q):
                take(dve, oh_free[q % 2])
                nc.vector.tensor_copy(idx[:, q, :], src_t[:, bass.ds((it + 1) * CH + q * GT, GT)])\
                  .then_inc(idx_full[q], 1)

            def add_out(start, q, t):
                b, at = q // 2 % 2, (q % 2 * GT + t) * WIN
                here = out_t[:, bass.ds(start[t], WIN)]
                take(dve, added)
                nc.vector.tensor_tensor(here, here, ps_o[b][:, at:at + WIN], ALU.add).then_inc(added, 1)

            def slot(it, q):
                if q < G:
                    refill(it, q)
                    cells((it + 1) * CH, q)
                if q >= 2:
                    start = load_bases(dve, it * CH + (q - 2) * GT, GT)
                    if q % 2 == 0:
                        take(dve, o_full[(q - 2) // 2 % 2])
                        dve.sem_inc(sums_free[(q - 2) // 2 % 2], 1)
                for t in range(GT):
                    if q + 2 < G:
                        weigh(it, q + 2, t)
                    if q >= 2:
                        add_out(start, q - 2, t)
                if q >= 2 and q % 2 == 1:
                    dve.wait_ge(added, 1)
                    dve.sem_inc(o_free[(q - 2) // 2 % 2], 1)

            def layer_sums():
                first_windows()
                take(dve, root_added)
                with dve.Fori(0, count_of):
                    dve.sem_inc(windows_full, 1)
                    keys()
                    for q in range(G):
                        cells(0, q)
                    weights(0)
                    with dve.Fori(0, NI) as it:
                        for q in range(2):
                            for t in range(GT):
                                weigh(it, q, t)
                        for q in range(G + 2):
                            slot(it, q)
                        weights((it + 1) * CH)
                    take(dve, windows_free)
                    next_windows()
                dve.wait_ge(added, 1)
                for s in sums_ready:
                    dve.sem_inc(s, 1)

            dve.sem_inc(added, 1)
            with dve.Fori(0, L - 1):
                layer_sums()
                for n in range(0, NB, 2):
                    take(dve, r_full_dve[0])
                    part, tiles = tile_rows(n * TB), len(blocks_of(n))
                    done(nc.vector.tensor_scalar(
                        rows[0:part, n * TB:n * TB + tiles, :],
                        ps_r[0][0:part, 0:tiles * D].rearrange("p (t d) -> p t d", d=D), 0.0, None, ALU.max))
                    dve.sem_inc(r_free[0], 1)
                    dve.sem_inc(rows_full[0], 1)
            layer_sums()

            def add_residual(n):
                b, part, tiles = n % 2, tile_rows(n * TB), len(blocks_of(n))
                take(dve, r_full_dve[b])
                nc.vector.tensor_tensor(
                    rows[0:part, n * TB:n * TB + tiles, :], x_again[0:part, n * TB:n * TB + tiles, :],
                    ps_r[b][0:part, 0:tiles * D].rearrange("p (t d) -> p t d", d=D), ALU.add)\
                    .then_inc(residual_in, 1)

            def take_stats(n):
                dve.wait_ge(residual_in, n + 1)
                dve.sem_inc(r_free[n % 2], 1)
                for s in blocks_of(n):
                    part = tile_rows(s)
                    ins = nc.vector.bn_stats(stats[0:part, s, :], rows[0:part, s, :])
                ins.then_inc(stats_in, 1)

            def take_moments(n):
                dve.wait_ge(stats_in, n + 1)
                for s in blocks_of(n):
                    part = tile_rows(s)
                    ins = nc.vector.bn_aggr(moments[0:part, s, :], stats[0:part, s, :])
                ins.then_inc(var_ready, 1)

            def invert(n):
                dve.wait_ge(std_ready, n + 1)
                part, lo, hi = tile_rows(n * TB), n * TB, n * TB + len(blocks_of(n))
                nc.vector.reciprocal(rstd[0:part, lo:hi], std[0:part, lo:hi]).then_inc(rstd_ready, 1)
                dve.wait_ge(rstd_ready, n + 1)
                nc.vector.scalar_tensor_tensor(shift[0:part, lo:hi], moments[0:part, lo:hi, 0], -1.0,
                                               rstd[0:part, lo:hi], ALU.mult, ALU.mult)\
                    .then_inc(shift_ready, 1)

            dve.wait_ge(x_in, 64)
            for n in range(NB + 3):
                if n < NB:
                    add_residual(n)
                if 0 <= n - 1 < NB:
                    take_stats(n - 1)
                if 0 <= n - 2 < NB:
                    take_moments(n - 2)
                if 0 <= n - 3:
                    invert(n - 3)

        @block.scalar
        def _(act):
            def done(ins):
                ins.then_inc(act_step, 1)
                act.wait_ge(act_step, 1)
                act.sem_inc(act_step, -1)

            for b in range(2):
                act.sem_inc(a_free[b], 1)

            def to_columns(to):
                for b in range(2):
                    lo, hi = b * BLK, min((b + 1) * BLK, RAW * P)
                    take(act, r_full_act[b])
                    done(nc.scalar.copy(to[:, lo:hi], ps_r[b][:, 0:hi - lo]))
                    act.sem_inc(r_free[b], 1)

            to_columns(brel_t)
            to_columns(cell_t)
            act.sem_inc(bkt_rows_ready, 1)
            to_columns(src_t)
            for q in range(G):
                nc.scalar.copy(idx[:, q, :], src_t[:, q * GT:(q + 1) * GT]).then_inc(idx_full[q], 1)
            to_columns(rel_t)
            to_columns(typ_t)
            act.sem_inc(index_ready, 1)
            for n in range(NB):
                b, cols = n % 2, block_cols(n)
                take(act, r_full_act[b])
                done(nc.scalar.copy(h_t[:, n * BLK:n * BLK + cols], ps_r[b][:, 0:cols]))
                act.sem_inc(r_free[b], 1)
            act.sem_inc(h_ready, 1)
            take(act, passes_ready[1])
            count_of = load_passes(act)
            done(nc.scalar.activation(out_t[:, N:NPAD], ident[:, 0:WIN], ACT.Copy, scale=0.0))

            def turned(q):
                b = q % 2
                take(act, r_full_act[b])
                act.sem_inc(cell_free[b], 1)
                take(act, turned_free[b])
                done(nc.scalar.copy(oh_cell_t[:, b, :], ps_r[b][:, :]))
                act.sem_inc(r_free[b], 1)
                act.sem_inc(turned_full[b], 1)

            def evacuate(q):
                a, b, at = q % 2, q // 2 % 2, q % 2 * GT
                take(act, a_full[a])
                act.sem_inc(oh_free[a], 1)
                if q % 2 == 0:
                    take(act, sums_free[b])
                done(nc.scalar.copy(sums[:, b, :, at:at + GT, :].rearrange("p r t w -> p t r w"),
                                    ps_a[a][:, :].rearrange("p (t r w) -> p t r w", r=R, t=GT)))
                act.sem_inc(a_free[a], 1)
                if q % 2 == 1:
                    act.sem_inc(sums_full[b], 1)

            def root_and_sums(last=False):
                for n in range(NB):
                    b, cols = n % 2, block_cols(n)
                    take(act, r_full_act[b])
                    done(nc.scalar.activation(out_t[:, n * BLK:n * BLK + cols], ps_r[b][:, 0:cols],
                                              ACT.Identity, bias=bias[:, 0:1]))
                    act.sem_inc(r_free[b], 1)
                act.sem_inc(root_added, 1)
                if last:
                    act.sem_inc(h_free, 1)
                with act.Fori(0, count_of):
                    for q in range(G):
                        turned(q)
                    with act.Fori(0, NI):
                        evacuate(0)
                        for q in range(G):
                            if q + 1 < G:
                                evacuate(q + 1)
                            if q >= 1:
                                turned(q - 1)
                        turned(G - 1)

            with act.Fori(0, L - 1):
                root_and_sums()
                take(act, sums_ready[1])
                for n in range(1, NB, 2):
                    take(act, r_full_act[1])
                    part, tiles = tile_rows(n * TB), len(blocks_of(n))
                    done(nc.scalar.activation(
                        rows[0:part, n * TB:n * TB + tiles, :],
                        ps_r[1][0:part, 0:tiles * D].rearrange("p (t d) -> p t d", d=D), ACT.Relu))
                    act.sem_inc(r_free[1], 1)
                    act.sem_inc(rows_full[1], 1)
                done(nc.scalar.activation(h_t[:, 0:N], out_t[:, 0:N], ACT.Relu))
                act.sem_inc(h_ready, 1)
            root_and_sums(last=True)
            for n in range(NB + 1):
                if n < NB:
                    part, lo, hi = tile_rows(n * TB), n * TB, n * TB + len(blocks_of(n))
                    act.wait_ge(var_ready, n + 1)
                    nc.scalar.activation(std[0:part, lo:hi], moments[0:part, lo:hi, 1], ACT.Sqrt,
                                         bias=eps[0:part, 0:1]).then_inc(std_ready, 1)
                if n > 0:
                    act.wait_ge(shift_ready, n)
                    for s in blocks_of(n - 1):
                        part = tile_rows(s)
                        ins = nc.scalar.activation(rows[0:part, s, :], rows[0:part, s, :], ACT.Identity,
                                                   bias=shift[0:part, s:s + 1], scale=rstd[0:part, s:s + 1])
                    ins.then_inc(out_full, 1)

        @block.tensor
        def _(pe):
            for b in range(2):
                pe.sem_inc(r_free[b], 1)
                pe.sem_inc(sums_free[b], 1)
                pe.sem_inc(o_free[b], 1)
                pe.sem_inc(turned_free[b], 1)
            pe.sem_inc(cell_free[0], 1)
            pe.sem_inc(weights_free, 1)
            pe.sem_inc(bkt_free, 1)
            pe.wait_ge(const_ready, 3)
            take(pe, low_ready)
            for cols in (low, high):
                for b in range(2):
                    take(pe, r_free[b])
                    for n in range(b * TB, min((b + 1) * TB, RAW)):
                        ins = nc.tensor.matmul(ps_r[b][0:1, (n - b * TB) * P:(n - b * TB + 1) * P],
                                               cols[:, n:n + 1], ident[:, :], start=True, stop=True)
                    ins.then_inc(r_full_dve[b], 1)

            def to_columns(raw):
                for b in range(2):
                    take(pe, r_free[b])
                    for n in range(b * TB, min((b + 1) * TB, RAW)):
                        ins = nc.tensor.transpose(ps_r[b][:, (n - b * TB) * P:(n - b * TB + 1) * P],
                                                  raw[:, n, :], ident[:, :])
                    ins.then_inc(r_full_act[b], 1)

            take(pe, bkt_ready)
            to_columns(f_bkt)
            to_columns(f_cell)
            take(pe, src_ready)
            to_columns(f_src)
            take(pe, passes_ready[0])
            count_of = load_passes(pe)
            counts_of = load_value(pe, passes[0:1, 1:2], 1, BUCKETS, "a span of buckets over 8")[0]

            nc.tensor.matmul(ps_c[:, :], zeros[:, 0:P], zeros[:, :], start=True, stop=False)
            with pe.Fori(0, counts_of):
                take(pe, windows_full)
                with pe.Fori(0, NI) as it:
                    take(pe, bkt_full)
                    for q in range(G):
                        b = q % 2
                        start = load_buckets(pe, it * CH + q * GT, GT)
                        take(pe, cell_full[b])
                        for t in range(GT):
                            ins = nc.tensor.matmul(ps_c[:, bass.ds(start[t], BWIN)], oh_cell[:, b, t, :],
                                                   oh_bkt[:, q * GT + t, :], start=False, stop=False)
                        if q + 1 < G:
                            ins.then_inc(cell_free[b], 1)
                        else:
                            ins.then_inc(bkt_free, 1)
                pe.sem_inc(windows_free, 1)
            nc.tensor.matmul(ps_c[:, :], zeros[:, 0:P], zeros[:, :], start=False, stop=True)\
                .then_inc(count_full, 1)
            take(pe, rel_ready)
            to_columns(f_dst)
            to_columns(f_typ)
            pe.wait_ge(x_in, 32)
            for n in range(NB):
                b = n % 2
                take(pe, r_free[b])
                for s in blocks_of(n):
                    part, at = tile_rows(s), (s - n * TB) * P
                    ins = nc.tensor.transpose(ps_r[b][:, at:at + part], x_rows[0:part, s, :],
                                              ident[0:part, 0:part])
                ins.then_inc(r_full_act[b], 1)
            take(pe, parts_ready)

            def turn(q):
                b = q % 2
                take(pe, cell_full[b])
                take(pe, r_free[b])
                for t in range(GT):
                    ins = nc.tensor.matmul(ps_r[b][:, t * P:(t + 1) * P], oh_cell[:, b, t, :], ident_bf[:, :],
                                           start=True, stop=True)
                ins.then_inc(r_full_act[b], 1)

            def look_up(start, q):
                b = q % 2
                bucket = load_buckets(pe, start + q * GT, GT)
                if q == 0:
                    take(pe, weights_free)
                take(pe, turned_full[b])
                for t in range(GT):
                    at = (q * GT + t) * 2 * PARTS
                    ins = nc.tensor.matmul(ps_w[:, at:at + 2 * PARTS], oh_cell_t[:, b, t * P:(t + 1) * P],
                                           inv_parts[:, bass.ds(bucket[t], 2), :].rearrange("p w k -> p (w k)"),
                                           start=True, stop=True)
                ins.then_inc(turned_free[b] if q + 1 < G else weights_full, 1)

            done_of = pe.alloc_register("gathers_done")
            pe.reg_mov(done_of, 0)

            def sum_edges(q, target):
                b = q % 2
                take(pe, oh_full[b])
                take(pe, a_free[b])
                pe.wait_ge(gathered[q], target)
                for t in range(GT):
                    ins = nc.tensor.matmul(ps_a[b][:, t * KEYS:(t + 1) * KEYS], ring[:, q, t, :],
                                           onehot[:, b, t, :], start=True, stop=True)
                ins.then_inc(a_full[b], 1)

            def apply_types(u):
                b = u % 2
                take(pe, sums_full[b])
                take(pe, o_free[b])
                for r in range(R):
                    ins = nc.tensor.matmul(ps_o[b][:, 0:PAIR * WIN], w_rel[:, r, :],
                                           sums[:, b, r, :, :].rearrange("p t w -> p (t w)"),
                                           start=(r == 0), stop=(r == R - 1))
                ins.then_inc(o_full[b], 1)

            def root_and_sums():
                take(pe, w_ready)
                take(pe, h_ready)
                for n in range(NB):
                    b, cols = n % 2, block_cols(n)
                    take(pe, r_free[b])
                    nc.tensor.matmul(ps_r[b][:, 0:cols], w_root[:, :], h_t[:, n * BLK:n * BLK + cols],
                                     start=True, stop=True).then_inc(r_full_act[b], 1)
                with pe.Fori(0, count_of):
                    take(pe, windows_full)
                    for q in range(G):
                        turn(q)
                        if q > 0:
                            look_up(0, q - 1)
                    look_up(0, G - 1)
                    with pe.Fori(0, NI) as it:
                        pe.reg_add(done_of, done_of, GT * 16)
                        target = pe.snap(done_of)
                        sum_edges(0, target)
                        for q in range(G):
                            if q + 1 < G:
                                sum_edges(q + 1, target)
                            if q % 2 == 1:
                                apply_types(q // 2)
                            if q >= 1:
                                turn(q - 1)
                            if q >= 2:
                                look_up((it + 1) * CH, q - 2)
                        turn(G - 1)
                        look_up((it + 1) * CH, G - 2)
                        look_up((it + 1) * CH, G - 1)
                    pe.sem_inc(windows_free, 1)

            with pe.Fori(0, L - 1):
                root_and_sums()
                take(pe, sums_ready[0])
                pe.sem_inc(w_used, 1)
                for n in range(NB):
                    b = n % 2
                    take(pe, r_free[b])
                    for s in blocks_of(n):
                        part, at = tile_rows(s), (s - n * TB) * D
                        ins = nc.tensor.transpose(ps_r[b][0:part, at:at + D],
                                                  out_t[:, s * P:s * P + part], ident[:, :])
                    ins.then_inc((r_full_dve, r_full_act)[b][b], 1)
            root_and_sums()
            take(pe, sums_ready[0])
            for n in range(NB):
                b = n % 2
                take(pe, r_free[b])
                for s in blocks_of(n):
                    part, at = tile_rows(s), (s - n * TB) * D
                    ins = nc.tensor.transpose(ps_r[b][0:part, at:at + D],
                                              out_t[:, s * P:s * P + part], ident[:, :])
                ins.then_inc(r_full_dve[b], 1)


_INS = ["x", "src", "dst", "edge_type_8", "L0_gnn_Ws", "L0_gnn_W_roots", "L0_gnn_bs"]


def kernel(**inputs):
    import numpy as _np
    import concourse.bacc as _bacc
    from concourse import mybir as _mybir
    from concourse.bass_utils import run_bass_kernel_spmd as _run

    nc = _bacc.Bacc("TRN2", target_bir_lowering=False, num_devices=1)
    arrays, args = {}, []
    for name in _INS:
        a = _np.ascontiguousarray(inputs[name])
        arrays[f"in_{name}"] = a
        args.append(nc.dram_tensor(f"in_{name}", a.shape, _mybir.dt.from_np(a.dtype), kind="ExternalInput").ap())
    out = nc.dram_tensor("out_rows", (N, D), F32, kind="ExternalOutput").ap()
    table = nc.dram_tensor("node_table", (N, D), F32, kind="Internal").ap()
    rgcn(nc, *args, out, table)
    r = _run(nc, [arrays], core_ids=[0])
    return r.results[0]["out_rows"]
```

```python
from contextlib import ExitStack

import concourse.bass as bass
from concourse import mybir

F32 = mybir.dt.float32
BF16 = mybir.dt.bfloat16
I32 = mybir.dt.int32
ALU = mybir.AluOpType
ACT = mybir.ActivationFunctionType
AX = mybir.AxisListType

N = 6250
E = 106250
D = 128
R = 8
L = 3
P = 128
EPS = 1e-5

RAW = -(-E // (P * P))
FULL = E // (P * P)
TAIL = (E - FULL * P * P) // P
REST = E - FULL * P * P - TAIL * P
CT = 16
GT = 4
G = 26
LOOKS = [0, 4, 8, 13, 17, 21, 26]
AHEAD = G // 2
PAIR = 2 * GT
NU = -(-E // (P * CT))
UNITS = 4
NU += -NU % UNITS
NT = NU * CT
assert NT % (G * GT) == 0
NL = NT // (G * GT)
WIN = 16
KEYS = R * WIN
BN = 8
CELLS = BN * R
BUCKETS = -(-N // BN)
NEAR = WIN // BN + 1
BWIN = 32
PARTS = 3
NO_TYPE = 2000
BLK = 512
NB = -(-N // BLK)
NS = -(-N // P)
TB = BLK // P
BANKS = 6
PER = NU // UNITS // NB
NTAIL = N - (NS - 1) * P
NPAD = N + WIN
BPAD = BUCKETS + BWIN


def rgcn(nc, x, src, dst, typ, Ws, Wr, bs, out, table):
    with ExitStack() as ctx:
        def sb(name, shape, dt):
            return ctx.enter_context(nc.sbuf_tensor(name, shape, dt))

        def sem(name):
            return ctx.enter_context(nc.semaphore(name))

        def pair(name):
            return [sem(f"{name}{i}") for i in range(2)]

        ident = sb("ident", [P, P], F32)
        ident_bf = sb("ident_bf", [P, P], BF16)
        zeros = sb("zeros", [P, P], BF16)
        iota_1 = sb("iota_1", [P, P], F32)
        iota_bf = sb("iota_bf", [P, CELLS, CT], BF16)
        ones = sb("ones", [1, P], F32)
        eps = sb("eps", [P, 1], F32)
        low = sb("low", [P, RAW], F32)
        low_i = sb("low_i", [P, RAW], I32)
        low_bkt = sb("low_bkt", [P, RAW], I32)
        high = sb("high", [P, RAW], F32)
        span = sb("span", [P, RAW], F32)
        most_span = sb("most_span", [P, 1], F32)
        src_t = sb("src_t", [P, max(RAW * P, NT + G * GT)], I32)
        rel_t = sb("rel_t", [P, RAW * P], F32)
        typ_t = sb("typ_t", [P, RAW * P], F32)
        cell_t = sb("cell_t", [P, RAW * P], BF16)
        brel_t = sb("brel_t", [P, RAW * P], F32)
        rel_k = sb("rel_k", [P, NT], F32)
        brel_k = sb("brel_k", [P, NT + AHEAD * GT], F32)
        crel_bf = sb("crel_bf", [P, NT], BF16)
        key = sb("key", [P, NT], F32)
        weight = sb("weight", [P, NT + AHEAD * GT], F32)
        crel_k = weight[:, 0:NT]
        over_f = key[0:1, :]
        count_k = sb("count_k", [1, UNITS + NU], I32)
        base_0 = sb("base_0", [1, NT + AHEAD * GT], I32)
        base_k = sb("base_k", [1, NT + AHEAD * GT], I32)
        bucket_0 = sb("bucket_0", [1, NT + AHEAD * GT], I32)
        bucket_k = sb("bucket_k", [1, NT + AHEAD * GT], I32)
        span_i = sb("span_i", [1, 6], I32)
        passes = sb("passes", [1, 4], I32)
        idx = sb("idx", [P, G, GT], I32)
        ring = sb("ring", [P, G, GT, D], F32)
        onehot = sb("onehot", [P, 2, GT, KEYS], F32)
        oh_cell = sb("oh_cell", [P, 2, CELLS, GT], BF16)
        oh_cell_t = sb("oh_cell_t", [CELLS, 2, GT * P], BF16)
        count_cell = sb("count_cell", [P, UNITS, CELLS, CT], BF16)
        count_bkt = sb("count_bkt", [P, UNITS, BWIN, CT], BF16)
        oh_bkt = sb("oh_bkt", [P, G * GT, NEAR], BF16)
        picked = sb("picked", [P, G * GT, NEAR, PARTS], F32)
        sums = sb("sums", [D, 2, R, PAIR, WIN], F32)
        inverse = sb("inverse", [CELLS, BPAD], F32)
        inv_rest = sb("inv_rest", [CELLS, BPAD], F32)
        inv_parts = sb("inv_parts", [CELLS, BPAD, PARTS], BF16)
        with ExitStack() as early:
            def sb_early(name, shape, dt):
                return early.enter_context(nc.sbuf_tensor(name, shape, dt))

            iota_i = sb_early("iota_i", [P, P], I32)
            raw_src = sb_early("raw_src", [P, RAW, P], I32)
            raw_dst = sb_early("raw_dst", [P, RAW, P], I32)
            raw_typ = sb_early("raw_typ", [P, RAW, P], I32)
            bkt_i = sb_early("bkt_i", [P, RAW, P], I32)
            node_i = raw_dst
        h_t = sb("h_t", [D, NB * BLK], F32)
        out_t = sb("out_t", [D, NS * P], F32)
        slots = ring[:, :, :, :].rearrange("p g t d -> p (g t) d")
        rows = slots[:, 0:NB * TB, :]
        f_src, f_dst, f_typ, f_bkt, f_cell = (
            slots[:, G * GT - (n + 1) * RAW:G * GT - n * RAW, :] for n in range(5))
        x_rows = out_t[:, :].rearrange("p (t d) -> p t d", d=D)
        x_again = h_t[:, 0:NS * P].rearrange("p (t d) -> p t d", d=D)
        w_rel = sb("w_rel", [D, R, D], F32)
        w_root = sb("w_root", [D, D], F32)
        bias = sb("bias", [D, 1], F32)
        stats = sb("stats", [P, NS, 6], F32)
        moments = sb("moments", [P, NB * TB, 2], F32)
        std = sb("std", [P, NB * TB], F32)
        rstd = sb("rstd", [P, NB * TB], F32)
        shift = sb("shift", [P, NB * TB], F32)

        ps_a = [ctx.enter_context(nc.psum_tensor(f"ps_a{i}", [P, BLK], F32)) for i in range(2)]
        ps_o = [ctx.enter_context(nc.psum_tensor(f"ps_o{i}", [P, BLK], F32)) for i in range(2)]
        ps_r = [ctx.enter_context(nc.psum_tensor(f"ps_r{i}", [P, BLK], F32)) for i in range(2)]
        ps_c = ps_a + ps_o
        ps_w = [ctx.enter_context(nc.psum_tensor(f"ps_w{i}", [P, BLK], F32)) for i in range(2)]

        dst_in = sem("dst_in")
        typ_in = sem("typ_in")
        src_in = sem("src_in")
        x_in = sem("x_in")
        w_in = sem("w_in")
        table_in = sem("table_in")
        out_in = sem("out_in")
        const_step = sem("const_step")
        const_ready = sem("const_ready")
        raw_cleared = sem("raw_cleared")
        dve_step = sem("dve_step")
        act_step = sem("act_step")
        low_ready = sem("low_ready")
        bkt_ready = sem("bkt_ready")
        src_ready = sem("src_ready")
        rel_ready = sem("rel_ready")
        typ_ready = sem("typ_ready")
        bkt_rows_ready = sem("bkt_rows_ready")
        passes_ready = [sem(f"passes_ready_{e}") for e in ("pe", "act", "pool")]
        reach_ready = sem("reach_ready")
        base_ready = sem("base_ready")
        first_ready = sem("first_ready")
        unit_full = [sem(f"unit_full{u}") for u in range(UNITS)]
        unit_free = [sem(f"unit_free{u}") for u in range(UNITS)]
        counted = sem("counted")
        windows_free = sem("windows_free")
        cell_full = pair("cell_full")
        cell_free = pair("cell_free")
        turned_full = pair("turned_full")
        turned_free = pair("turned_free")
        windows_full = sem("windows_full")
        weights_full = pair("weights_full")
        weights_free = pair("weights_free")
        weights_step = sem("weights_step")
        h_ready = sem("h_ready")
        w_ready = sem("w_ready")
        w_used = sem("w_used")
        root_added = sem("root_added")
        sums_ready = [sem(f"sums_ready_{e}") for e in ("pe", "act")]
        rows_full = pair("rows_full")
        table_ready = sem("table_ready")
        idx_full = [sem(f"idx_full{q}") for q in range(G)]
        gathered = [sem(f"gathered{q}") for q in range(G)]
        block_full = [sem(f"block_full{i}") for i in range(BANKS)]
        block_free = [sem(f"block_free{i}") for i in range(BANKS)]
        oh_full = pair("oh_full")
        oh_free = pair("oh_free")
        a_full = pair("a_full")
        a_free = sem("a_free")
        sums_full = pair("sums_full")
        sums_free = pair("sums_free")
        added = sem("added")
        o_full = pair("o_full")
        o_free = pair("o_free")
        r_full_act = pair("r_full_act")
        r_full_dve = pair("r_full_dve")
        r_free = pair("r_free")
        h_free = sem("h_free")
        stats_in = sem("stats_in")
        var_ready = sem("var_ready")
        std_ready = sem("std_ready")
        rstd_ready = sem("rstd_ready")
        shift_ready = sem("shift_ready")
        out_full = sem("out_full")

        def take(eng, credit):
            eng.wait_ge(credit, 1)
            eng.sem_inc(credit, -1)

        def load_value(eng, ap, lo, hi, why):
            _, v = nc.values_load_multi_w_load_instructions(
                ap, engines=[eng.engine], min_val=lo, max_val=hi, skip_runtime_bounds_check_because=why)
            return v

        def load_passes(eng):
            return load_value(eng, passes[0:1, 0:1], 1, BUCKETS + 1, "a span of nodes over the window")[0]

        def load_bases(eng, start, n):
            return load_value(eng, base_k[0:1, bass.ds(start, n)], 0, N, "the chip clamps them to N")

        def load_buckets(eng, start, n):
            return load_value(eng, bucket_k[0:1, bass.ds(start, n)], 0, BUCKETS,
                              "the chip clamps them to the number of buckets")

        def block_cols(n):
            return min(BLK, N - n * BLK)

        def tile_rows(n):
            return min(P, N - n * P)

        def blocks_of(n):
            return range(n * TB, min((n + 1) * TB, NS))

        banks = ps_r + ps_a + ps_o

        block = ctx.enter_context(nc.Block())

        @block.sync
        def _(sp):
            cut = FULL * P * P
            sp.wait_ge(raw_cleared, 3)
            for raw, flat, landed in ((raw_dst, dst, dst_in), (raw_src, src, src_in), (raw_typ, typ, typ_in)):
                sp.dma_start(raw[:, 0:FULL, :], flat[0:cut].rearrange("(b p e) -> p b e", p=P, e=P))\
                  .then_inc(landed, 16)
                sp.dma_start(raw[0:TAIL, FULL, :],
                             flat[cut:cut + TAIL * P].rearrange("(p e) -> p e", e=P))\
                  .then_inc(landed, 16)
                sp.dma_start(raw[TAIL:TAIL + 1, FULL, 0:REST],
                             flat[E - REST:E].rearrange("(p e) -> p e", p=1)).then_inc(landed, 16)
                if raw is raw_dst:
                    sp.dma_start(raw[TAIL:TAIL + 1, FULL, REST:P],
                                 flat[E - (P - REST):E].rearrange("(p e) -> p e", p=1)).then_inc(landed, 16)
                    for tile in range(TAIL + 1, NT - FULL * P):
                        sp.dma_start(raw[tile:tile + 1, FULL, :],
                                     flat[E - P:E].rearrange("(p e) -> p e", p=1)).then_inc(landed, 16)

            whole = (NS - 1) * P
            sp.dma_start(x_rows[:, 0:NS - 1, :], x[0:whole, :].rearrange("(t p) d -> p t d", p=P))\
              .then_inc(x_in, 16)
            sp.dma_start(x_rows[0:NTAIL, NS - 1, :], x[whole:N, :]).then_inc(x_in, 16)

            def load_weights(layer, landed):
                sp.dma_start(w_rel[:, :, :], Ws[bass.ds(layer, 1), :, :, :].rearrange("l r k d -> k (l r) d"))\
                  .then_inc(w_in, 16)
                sp.dma_start(w_root[:, :], Wr[bass.ds(layer, 1), :, :].rearrange("l k d -> (l k) d"))\
                  .then_inc(w_in, 16)
                sp.dma_start(bias[:, :], bs[bass.ds(layer, 1), :].rearrange("l d -> d l"))\
                  .then_inc(w_in, 16)
                sp.wait_ge(w_in, landed)
                sp.sem_inc(w_ready, 1)

            load_weights(0, 48)
            with sp.Fori(1, L) as layer:
                for n in range(NB):
                    take(sp, rows_full[n % 2])
                    lo, cols = n * BLK, block_cols(n)
                    if cols == BLK:
                        sp.dma_start(table[lo:lo + BLK, :].rearrange("(t p) d -> p t d", p=P),
                                     rows[:, n * TB:(n + 1) * TB, :]).then_inc(table_in, 16)
                    else:
                        sp.dma_start(table[lo:N, :], rows[0:cols, n * TB, :]).then_inc(table_in, 16)
                sp.wait_ge(table_in, layer * (16 * NB))
                sp.sem_inc(table_ready, 1)
                take(sp, w_used)
                load_weights(layer, layer * 48 + 48)
            take(sp, h_free)
            sp.dma_start(x_again[:, 0:NS - 1, :], x[0:whole, :].rearrange("(t p) d -> p t d", p=P))\
              .then_inc(x_in, 16)
            sp.dma_start(x_again[0:NTAIL, NS - 1, :], x[whole:N, :]).then_inc(x_in, 16)
            for n in range(NB):
                take(sp, out_full)
                sp.sem_inc(block_free[n % BANKS], 1)
                lo, cols = n * BLK, block_cols(n)
                if cols == BLK:
                    sp.dma_start(out[lo:lo + BLK, :].rearrange("(t p) d -> p t d", p=P),
                                 rows[:, n * TB:(n + 1) * TB, :]).then_inc(out_in, 16)
                else:
                    sp.dma_start(out[lo:N, :], rows[0:cols, n * TB, :]).then_inc(out_in, 16)
            sp.wait_ge(out_in, 16 * NB)

        @block.gpsimd
        def _(pool):
            nc.gpsimd.memset(raw_typ[:, FULL, :], NO_TYPE).then_inc(raw_cleared, 1)
            nc.gpsimd.memset(raw_dst[:, FULL, :], 0).then_inc(raw_cleared, 1)
            nc.gpsimd.memset(raw_src[:, FULL, :], 0).then_inc(raw_cleared, 1)
            nc.gpsimd.memset(ident[:, :], 0.0).then_inc(const_step, 1)
            nc.gpsimd.memset(eps[:, :], EPS).then_inc(const_ready, 1)
            nc.gpsimd.memset(zeros[:, :], 0.0)
            nc.gpsimd.memset(ones[:, :], 1.0)
            nc.gpsimd.memset(inverse[:, :], 0.0)
            nc.gpsimd.memset(count_k[:, :], 0)
            nc.gpsimd.iota(iota_i[:, :], pattern=[[1, P]], base=0, channel_multiplier=0).then_inc(const_ready, 1)
            pool.wait_ge(const_step, 1)
            nc.gpsimd.affine_select(out=ident[:, :], in_=ident[:, :], compare_op=ALU.not_equal, fill=1.0,
                                    base=0, pattern=[[-1, P]], channel_multiplier=1).then_inc(const_ready, 1)

            def gather_ring(source):
                for q in range(G):
                    take(pool, idx_full[q])
                    for t in range(GT):
                        nc.gpsimd.indirect_dma_start(
                            out=ring[:, q, t, :], out_offset=None, in_=source,
                            in_offset=bass.IndirectOffsetOnAxis(ap=idx[:, q, t:t + 1], axis=0))\
                          .then_inc(gathered[q], 16)

            gather_ring(x)
            take(pool, passes_ready[2])
            count_of = load_passes(pool)
            more = load_value(pool, passes[0:1, 2:3], NL - 1, (BUCKETS + 1) * NL, "NL or more, less one")[0]
            with pool.Fori(0, more):
                gather_ring(x)
            with pool.Fori(1, L):
                take(pool, table_ready)
                with pool.Fori(0, count_of):
                    with pool.Fori(0, NL):
                        gather_ring(table)

        @block.vector
        def _(dve):
            def done(ins):
                ins.then_inc(dve_step, 1)
                dve.wait_ge(dve_step, 1)
                dve.sem_inc(dve_step, -1)

            dve.wait_ge(const_ready, 3)
            nc.vector.tensor_scalar(iota_1[:, :], iota_i[:, :], 1.0, None, ALU.add)
            nc.vector.tensor_copy(iota_bf[:, :, :], iota_i[:, 0:CELLS].unsqueeze(2).broadcast_to([P, CELLS, CT]))
            nc.vector.tensor_copy(ident_bf[:, :], ident[:, :])
            dve.wait_ge(dst_in, 16 * (4 + NT - FULL * P - TAIL - 1))
            nc.vector.tensor_reduce(low_i[:, :], raw_dst[:, :, :], AX.X, ALU.min)
            done(nc.vector.tensor_reduce(high[:, :], raw_dst[:, :, :], AX.X, ALU.max))
            nc.vector.tensor_copy(low[:, :], low_i[:, :])
            nc.vector.tensor_scalar(low_bkt[:, :], low_i[:, :], BN.bit_length() - 1, None, ALU.arith_shift_right)
            done(nc.vector.tensor_tensor(span[:, :], high[:, :], low_i[:, :], ALU.subtract))
            done(nc.vector.tensor_reduce(most_span[:, :], span[:, :], AX.X, ALU.max))
            dve.sem_inc(low_ready, 1)
            nc.vector.tensor_scalar(bkt_i[:, :, :], raw_dst[:, :, :], BN.bit_length() - 1, None,
                                    ALU.arith_shift_right)
            done(nc.vector.tensor_tensor(f_dst[:, :, :], raw_dst[:, :, :],
                                         low_i[:, :].unsqueeze(2).broadcast_to([P, RAW, P]), ALU.subtract))
            dve.sem_inc(rel_ready, 1)
            nc.vector.tensor_scalar(node_i[:, :, :], raw_dst[:, :, :], BN - 1, None, ALU.bitwise_and)
            done(nc.vector.tensor_tensor(f_bkt[:, :, :], bkt_i[:, :, :],
                                         low_bkt[:, :].unsqueeze(2).broadcast_to([P, RAW, P]), ALU.subtract))
            dve.wait_ge(typ_in, 16 * 3)
            done(nc.vector.scalar_tensor_tensor(f_cell[:, :, :], node_i[:, :, :], float(R), raw_typ[:, :, :],
                                                ALU.mult, ALU.add))
            dve.sem_inc(bkt_ready, 1)
            for b in range(2):
                lo, hi = b * BLK, min((b + 1) * BLK, NT + AHEAD * GT)
                take(dve, r_full_dve[b])
                done(nc.vector.tensor_copy(base_0[0:1, lo:hi], ps_r[b][0:1, 0:hi - lo]))
                dve.sem_inc(r_free[b], 1)
            done(nc.vector.tensor_scalar(bucket_0[:, :], base_0[:, :], BN.bit_length() - 1, None,
                                         ALU.arith_shift_right))
            dve.sem_inc(base_ready, 1)
            by_unit = bucket_0[:, 0:NT].rearrange("o (i c) -> o i c", c=CT)
            first = count_k[:, UNITS:UNITS + NU]
            done(nc.vector.tensor_reduce(first, by_unit, AX.X, ALU.min))
            done(nc.vector.tensor_tensor(over_f[:, :].rearrange("o (i c) -> o i c", c=CT), by_unit,
                                         first.unsqueeze(2).broadcast_to([1, NU, CT]), ALU.subtract))
            dve.sem_inc(reach_ready, 1)
            take(dve, r_full_dve[0])
            nc.vector.tensor_reduce(span_i[0:1, 0:1], ps_r[0][0:1, 0:P], AX.X, ALU.max)
            done(nc.vector.tensor_reduce(span_i[0:1, 2:3], over_f[0:1, :], AX.X, ALU.max))
            dve.sem_inc(r_free[0], 1)
            nc.vector.tensor_scalar(span_i[0:1, 1:2], span_i[0:1, 0:1], WIN.bit_length() - 1, None,
                                    ALU.arith_shift_right)
            done(nc.vector.scalar_tensor_tensor(span_i[0:1, 4:5], span_i[0:1, 2:3], float(BN),
                                                span_i[0:1, 0:1], ALU.mult, ALU.add))
            nc.vector.tensor_scalar(passes[:, 0:1], span_i[0:1, 1:2], 1.0, None, ALU.add)
            done(nc.vector.tensor_scalar(span_i[0:1, 5:6], span_i[0:1, 4:5], float(BN - 1), None, ALU.add))
            nc.vector.tensor_scalar(passes[:, 2:3], span_i[0:1, 1:2], float(NL), float(NL - 1),
                                    ALU.mult, ALU.add)
            done(nc.vector.tensor_scalar(span_i[0:1, 3:4], span_i[0:1, 5:6],
                                         (BWIN * BN).bit_length() - 1, None, ALU.arith_shift_right))
            nc.vector.tensor_scalar(passes[:, 1:2], span_i[0:1, 3:4], 1.0, None, ALU.add)
            done(nc.vector.tensor_scalar(passes[:, 3:4], span_i[0:1, 3:4], float(NU // UNITS),
                                         float(NU // UNITS - (NB - 1) * PER), ALU.mult, ALU.add))
            for s in passes_ready:
                dve.sem_inc(s, 1)
            count_of = load_passes(dve)
            counts_of = load_value(dve, passes[0:1, 1:2], 1, BUCKETS, "buckets over a window's")[0]

            def cells(start, q):
                b = q % 2
                take(dve, cell_free[b])
                nc.vector.tensor_tensor(
                    oh_cell[:, b, :, :],
                    cell_t[:, bass.ds(start + q * GT, GT)].unsqueeze(1).broadcast_to([P, CELLS, GT]),
                    iota_bf[:, :, 0:GT], ALU.is_equal).then_inc(cell_full[b], 1)

            def load_units(entry, n):
                return load_value(dve, count_k[0:1, bass.ds(entry, n)], 0, BUCKETS,
                                  "the chip clamps them to the number of buckets")

            def add_counts(start, h):
                take(dve, unit_free[h])
                take(dve, counted)
                here = inverse[:, bass.ds(start, BWIN)]
                nc.vector.tensor_tensor(here, here, ps_c[h][0:CELLS, 0:BWIN], ALU.add).then_inc(counted, 1)

            take(dve, bkt_rows_ready)
            for b in range(2):
                lo, hi = b * BLK, min((b + 1) * BLK, NT)
                take(dve, r_full_dve[b])
                done(nc.vector.tensor_tensor(crel_k[:, lo:hi], brel_t[:, lo:hi], ps_r[b][:, 0:hi - lo], ALU.add))
                dve.sem_inc(r_free[b], 1)
            def first_windows():
                nc.vector.tensor_copy(base_k[:, :], base_0[:, :])
                nc.vector.tensor_copy(bucket_k[:, :], bucket_0[:, :])
                nc.vector.tensor_copy(brel_k[:, :], brel_t[:, 0:NT + AHEAD * GT])
                done(nc.vector.tensor_copy(rel_k[:, :], rel_t[:, 0:NT]))

            dve.sem_inc(counted, 1)
            with dve.Fori(0, counts_of):
                for h in range(UNITS):
                    nc.vector.memset(ps_c[h][0:CELLS, 0:BWIN], 0.0)
                done(nc.vector.tensor_copy(crel_bf[:, :], crel_k[:, :]))
                for h in range(UNITS):
                    dve.sem_inc(unit_free[h], 1)
                with dve.Fori(0, NU // UNITS) as it:
                    start = load_units(it * UNITS, UNITS)
                    for h in range(UNITS):
                        unit = it * UNITS + h
                        add_counts(start[h], h)
                        nc.vector.tensor_tensor(
                            count_bkt[:, h, :, :],
                            crel_bf[:, bass.ds(unit * CT, CT)].unsqueeze(1).broadcast_to([P, BWIN, CT]),
                            iota_bf[:, 0:BWIN, :], ALU.is_equal)
                        nc.vector.tensor_tensor(
                            count_cell[:, h, :, :],
                            cell_t[:, bass.ds(unit * CT, CT)].unsqueeze(1).broadcast_to([P, CELLS, CT]),
                            iota_bf[:, :, :], ALU.is_equal).then_inc(unit_full[h], 1)
                start = load_units(NU, UNITS)
                for h in range(UNITS):
                    add_counts(start[h], h)
                nc.vector.tensor_scalar(count_k[:, :], count_k[:, :], float(BWIN), float(BUCKETS),
                                        ALU.add, ALU.min)
                done(nc.vector.tensor_scalar(crel_k[:, :], crel_k[:, :], float(BWIN), None, ALU.subtract))
            dve.wait_ge(counted, 1)
            done(nc.vector.tensor_scalar(inverse[:, :], inverse[:, :], 1.0, None, ALU.max))
            done(nc.vector.reciprocal(inverse[:, :], inverse[:, :]))
            done(nc.vector.tensor_copy(inv_parts[:, :, 0], inverse[:, :]))
            done(nc.vector.tensor_tensor(inv_rest[:, :], inverse[:, :], inv_parts[:, :, 0], ALU.subtract))
            done(nc.vector.tensor_copy(inv_parts[:, :, 1], inv_rest[:, :]))
            done(nc.vector.tensor_tensor(inv_parts[:, :, 2], inv_rest[:, :], inv_parts[:, :, 1], ALU.subtract))

            def next_windows():
                nc.vector.tensor_scalar(base_k[:, :], base_k[:, :], float(WIN), float(N), ALU.add, ALU.min)
                nc.vector.tensor_scalar(bucket_k[:, :], bucket_k[:, :], float(WIN // BN), float(BUCKETS),
                                        ALU.add, ALU.min)
                nc.vector.tensor_scalar(brel_k[:, :], brel_k[:, :], float(WIN // BN), None, ALU.subtract)
                done(nc.vector.tensor_scalar(rel_k[:, :], rel_k[:, :], float(WIN), None, ALU.subtract))

            def which_bucket(start, tiles):
                nc.vector.tensor_tensor(
                    oh_bkt[:, 0:tiles, :],
                    brel_k[:, bass.ds(start, tiles)].unsqueeze(2).broadcast_to([P, tiles, NEAR]),
                    iota_bf[:, 0:NEAR, 0].unsqueeze(1).broadcast_to([P, tiles, NEAR]), ALU.is_equal)\
                    .then_inc(weights_step, 1)

            def pick(r, tiles):
                take(dve, weights_full[r])
                take(dve, weights_step)
                nc.vector.tensor_tensor(
                    picked[:, 0:tiles, :, :],
                    ps_w[r][:, 0:tiles * NEAR * PARTS].rearrange("p (c w k) -> p c w k", w=NEAR, k=PARTS),
                    oh_bkt[:, 0:tiles, :].unsqueeze(3).broadcast_to([P, tiles, NEAR, PARTS]), ALU.mult)\
                    .then_inc(weights_step, 1)

            def add_parts(start, r, tiles):
                take(dve, weights_step)
                dve.sem_inc(weights_free[r], 1)
                nc.vector.tensor_reduce(weight[:, bass.ds(start, tiles)],
                                        picked[:, 0:tiles, :, :].rearrange("p c w k -> p c (w k)"),
                                        AX.X, ALU.add).then_inc(weights_step, 1)

            def keys():
                done(nc.vector.tensor_tensor(key[:, :], typ_t[:, 0:NT], rel_k[:, :], ALU.add))
                done(nc.vector.scalar_tensor_tensor(key[:, :], rel_k[:, :], 0.0, key[:, :], ALU.is_ge, ALU.mult))
                done(nc.vector.scalar_tensor_tensor(key[:, :], rel_k[:, :], float(WIN), key[:, :],
                                                    ALU.is_lt, ALU.mult))

            def weigh(first, q, t):
                b, col = q % 2, first + (q * GT + t)
                ins = nc.vector.tensor_scalar(
                    onehot[:, b, t, :], iota_1[:, :], key[:, bass.ds(col, 1)],
                    weight[:, bass.ds(col, 1)], ALU.is_equal, ALU.mult)
                if t + 1 == GT:
                    ins.then_inc(oh_full[b], 1)

            def refill(first, q):
                take(dve, oh_free[q % 2])
                nc.vector.tensor_copy(idx[:, q, :], src_t[:, bass.ds(first + (G + q) * GT, GT)])\
                  .then_inc(idx_full[q], 1)

            def add_out(start, q, t):
                b, at = q // 2 % 2, (q % 2 * GT + t) * WIN
                here = out_t[:, bass.ds(start[t], WIN)]
                take(dve, added)
                nc.vector.tensor_tensor(here, here, ps_o[b][:, at:at + WIN], ALU.add).then_inc(added, 1)

            def slot(first, q):
                looks = q in LOOKS[:-1]
                if looks:
                    u = LOOKS.index(q) - 2
                    r, lo = u % 2, LOOKS[u % (len(LOOKS) - 1)]
                    tiles = (LOOKS[u % (len(LOOKS) - 1) + 1] - lo) * GT
                    at = first + ((lo if u >= 0 else lo - G) + AHEAD) * GT
                if q < G:
                    refill(first, q)
                    cells(first + AHEAD * GT, q)
                if looks:
                    which_bucket(at, tiles)
                if q >= 2:
                    start = load_bases(dve, first + (q - 2) * GT, GT)
                    if q % 2 == 0:
                        take(dve, o_full[(q - 2) // 2 % 2])
                        dve.sem_inc(sums_free[(q - 2) // 2 % 2], 1)
                for t in range(GT):
                    if q + 2 < G:
                        weigh(first, q + 2, t)
                    if q >= 2:
                        add_out(start, q - 2, t)
                    if looks and t == 0:
                        pick(r, tiles)
                    if looks and t == 2:
                        add_parts(at, r, tiles)
                if looks:
                    take(dve, weights_step)
                if q >= 2 and q % 2 == 1:
                    dve.wait_ge(added, 1)
                    dve.sem_inc(o_free[(q - 2) // 2 % 2], 1)

            def layer_sums():
                with dve.Fori(0, count_of):
                    dve.sem_inc(windows_full, 1)
                    keys()
                    first_looked = (LOOKS[4] - LOOKS[3]) * GT
                    for q in range(AHEAD):
                        cells(-GT, q + 1)
                        if q == LOOKS[4] - LOOKS[3] + 1:
                            which_bucket(0, first_looked)
                            pick(1, first_looked)
                            add_parts(0, 1, first_looked)
                            take(dve, weights_step)
                    take(dve, root_added)
                    with dve.Fori(0, NL) as it:
                        first = it * (G * GT)
                        for q in range(2):
                            for t in range(GT):
                                weigh(first, q, t)
                        for q in range(G + 2):
                            slot(first, q)
                    dve.wait_ge(added, 1)
                    for s in sums_ready:
                        dve.sem_inc(s, 1)
                    for r in range(2):
                        take(dve, weights_full[r])
                        dve.sem_inc(weights_free[r], 1)
                    take(dve, windows_free)
                    next_windows()

            dve.sem_inc(added, 1)
            take(dve, first_ready)
            with dve.Fori(0, L - 1):
                layer_sums()
                for n in range(1, NB, 2):
                    take(dve, block_full[n % BANKS])
                    part, tiles = tile_rows(n * TB), len(blocks_of(n))
                    done(nc.vector.tensor_scalar(
                        rows[0:part, n * TB:n * TB + tiles, :],
                        banks[n % BANKS][0:part, 0:tiles * D].rearrange("p (t d) -> p t d", d=D),
                        0.0, None, ALU.max))
                    dve.sem_inc(rows_full[1], 1)
                    dve.sem_inc(block_free[n % BANKS], 1)
                first_windows()
            layer_sums()

            def tile_of(n, s):
                return banks[n % BANKS][0:tile_rows(s), (s - n * TB) * D:(s - n * TB + 1) * D]

            def take_stats(n):
                take(dve, block_full[n % BANKS])
                for s in blocks_of(n):
                    ins = nc.vector.bn_stats(stats[0:tile_rows(s), s, :], tile_of(n, s))
                ins.then_inc(stats_in, 1)

            def take_moments(n):
                dve.wait_ge(stats_in, n + 1)
                for s in blocks_of(n):
                    part = tile_rows(s)
                    ins = nc.vector.bn_aggr(moments[0:part, s, :], stats[0:part, s, :])
                ins.then_inc(var_ready, 1)

            def invert(n):
                dve.wait_ge(std_ready, n + 1)
                part, lo, hi = tile_rows(n * TB), n * TB, n * TB + len(blocks_of(n))
                nc.vector.reciprocal(rstd[0:part, lo:hi], std[0:part, lo:hi]).then_inc(rstd_ready, 1)
                dve.wait_ge(rstd_ready, n + 1)
                nc.vector.scalar_tensor_tensor(shift[0:part, lo:hi], moments[0:part, lo:hi, 0], -1.0,
                                               rstd[0:part, lo:hi], ALU.mult, ALU.mult)\
                    .then_inc(shift_ready, 1)

            for n in range(NB + 2):
                if n < NB:
                    take_stats(n)
                if 0 <= n - 2:
                    invert(n - 2)
                if 0 <= n - 1 < NB:
                    take_moments(n - 1)

        @block.scalar
        def _(act):
            def done(ins):
                ins.then_inc(act_step, 1)
                act.wait_ge(act_step, 1)
                act.sem_inc(act_step, -1)

            act.sem_inc(a_free, 1)
            act.wait_ge(const_ready, 3)
            nc.scalar.activation(std[:, 0:1], eps[:, :], ACT.Sqrt)

            def to_columns(to):
                for b in range(2):
                    lo, hi = b * BLK, min((b + 1) * BLK, RAW * P)
                    take(act, r_full_act[b])
                    done(nc.scalar.copy(to[:, lo:hi], ps_r[b][:, 0:hi - lo]))
                    act.sem_inc(r_free[b], 1)

            act.wait_ge(src_in, 16 * 3)
            done(nc.scalar.copy(f_src[:, :, :], raw_src[:, :, :]))
            act.sem_inc(src_ready, 1)
            to_columns(src_t)
            early = G - -(-5 * RAW // GT)
            for q in range(early):
                nc.scalar.copy(idx[:, q, :], src_t[:, q * GT:(q + 1) * GT]).then_inc(idx_full[q], 1)
            act.wait_ge(typ_in, 16 * 3)
            done(nc.scalar.activation(f_typ[:, :, :], raw_typ[:, :, :], ACT.Copy, bias=1.0, scale=float(WIN)))
            act.sem_inc(typ_ready, 1)
            to_columns(rel_t)
            to_columns(brel_t)
            to_columns(cell_t)
            act.sem_inc(bkt_rows_ready, 1)
            to_columns(typ_t)
            for q in range(early, G):
                nc.scalar.copy(idx[:, q, :], src_t[:, q * GT:(q + 1) * GT]).then_inc(idx_full[q], 1)
            def root_block(n, b):
                cols = block_cols(n)
                take(act, r_full_act[b])
                done(nc.scalar.activation(out_t[:, n * BLK:n * BLK + cols], ps_r[b][:, 0:cols],
                                          ACT.Identity, bias=bias[:, 0:1]))
                act.sem_inc(r_free[b], 1)

            def clear_pad():
                done(nc.scalar.activation(out_t[:, N:NPAD], ident[:, 0:WIN], ACT.Copy, scale=0.0))

            nc.scalar.copy(src_t[:, NT:NT + G * GT], src_t[:, 0:G * GT])
            take(act, base_ready)
            nc.scalar.copy(base_k[:, :], base_0[:, :])
            nc.scalar.copy(bucket_k[:, :], bucket_0[:, :])
            nc.scalar.copy(brel_k[:, :], brel_t[:, 0:NT + AHEAD * GT])
            done(nc.scalar.copy(rel_k[:, :], rel_t[:, 0:NT]))
            act.sem_inc(first_ready, 1)
            for n in range(NB):
                b, cols = n % 2, block_cols(n)
                take(act, r_full_act[b])
                done(nc.scalar.copy(h_t[:, n * BLK:n * BLK + cols], ps_r[b][:, 0:cols]))
                act.sem_inc(r_free[b], 1)
            for n in range(NB):
                root_block(n, n % 2)
            clear_pad()
            take(act, passes_ready[1])
            count_of = load_passes(act)

            def turned(q, bank):
                b = q % 2
                take(act, r_full_act[b])
                act.sem_inc(cell_free[b], 1)
                take(act, turned_free[b])
                nc.scalar.copy(oh_cell_t[:, b, :], bank[0:CELLS, :]).then_inc(turned_full[b], 1)

            def evacuate(q):
                a, b, at = q % 2, q // 2 % 2, q % 2 * GT
                take(act, a_full[a])
                act.sem_inc(oh_free[a], 1)
                if q % 2 == 0:
                    take(act, sums_free[b])
                nc.scalar.copy(sums[:, b, :, at:at + GT, :].rearrange("p r t w -> p t r w"),
                               ps_a[a][:, :].rearrange("p (t r w) -> p t r w", r=R, t=GT))\
                  .then_inc(a_free if q % 2 == 0 else sums_full[b], 1)

            def layer_sums():
                with act.Fori(0, count_of):
                    act.sem_inc(root_added, 1)
                    for q in range(AHEAD):
                        turned(q + 1, banks[q % 4])
                    with act.Fori(0, NL):
                        evacuate(0)
                        for q in range(G):
                            if q + 1 < G:
                                evacuate(q + 1)
                            if q >= 1:
                                turned(q - 1, ps_r[(q - 1) % 2])
                        turned(G - 1, ps_r[1])
                    take(act, sums_ready[1])

            with act.Fori(0, L - 1):
                layer_sums()
                for n in range(0, NB, 2):
                    take(act, block_full[n % BANKS])
                    part, tiles = tile_rows(n * TB), len(blocks_of(n))
                    done(nc.scalar.activation(
                        rows[0:part, n * TB:n * TB + tiles, :],
                        banks[n % BANKS][0:part, 0:tiles * D].rearrange("p (t d) -> p t d", d=D), ACT.Relu))
                    act.sem_inc(rows_full[0], 1)
                    act.sem_inc(block_free[n % BANKS], 1)
                done(nc.scalar.activation(h_t[:, 0:N], out_t[:, 0:N], ACT.Relu))
                act.sem_inc(h_ready, 1)
                for n in range(NB):
                    root_block(n, n % 2)
                clear_pad()
            act.sem_inc(h_free, 1)
            layer_sums()
            for n in range(NB + 1):
                if n < NB:
                    part, lo, hi = tile_rows(n * TB), n * TB, n * TB + len(blocks_of(n))
                    act.wait_ge(var_ready, n + 1)
                    nc.scalar.activation(std[0:part, lo:hi], moments[0:part, lo:hi, 1], ACT.Sqrt,
                                         bias=eps[0:part, 0:1]).then_inc(std_ready, 1)
                if n > 0:
                    act.wait_ge(shift_ready, n)
                    for s in blocks_of(n - 1):
                        at, part = (s - (n - 1) * TB) * D, tile_rows(s)
                        ins = nc.scalar.activation(rows[0:part, s, :], banks[(n - 1) % BANKS][0:part, at:at + D],
                                                   ACT.Identity, bias=shift[0:part, s:s + 1],
                                                   scale=rstd[0:part, s:s + 1])
                    ins.then_inc(out_full, 1)

        @block.tensor
        def _(pe):
            for b in range(2):
                pe.sem_inc(r_free[b], 1)
                pe.sem_inc(sums_free[b], 1)
                pe.sem_inc(o_free[b], 1)
                pe.sem_inc(turned_free[b], 1)
                pe.sem_inc(cell_free[b], 1)
                pe.sem_inc(weights_free[b], 1)
            pe.wait_ge(const_ready, 3)
            def to_columns(raw):
                for b in range(2):
                    take(pe, r_free[b])
                    for n in range(b * TB, min((b + 1) * TB, RAW)):
                        ins = nc.tensor.transpose(ps_r[b][:, (n - b * TB) * P:(n - b * TB + 1) * P],
                                                  raw[:, n, :], ident[:, :])
                    ins.then_inc(r_full_act[b], 1)

            take(pe, src_ready)
            to_columns(f_src)
            take(pe, low_ready)
            for b in range(2):
                take(pe, r_free[b])
                for n in range(b * TB, min((b + 1) * TB, RAW)):
                    ins = nc.tensor.matmul(ps_r[b][0:1, (n - b * TB) * P:(n - b * TB + 1) * P],
                                           low[:, n:n + 1], ident[:, :], start=True, stop=True)
                ins.then_inc(r_full_dve[b], 1)
            take(pe, rel_ready)
            to_columns(f_dst)
            take(pe, bkt_ready)
            to_columns(f_bkt)
            to_columns(f_cell)
            take(pe, reach_ready)
            take(pe, r_free[0])
            nc.tensor.matmul(ps_r[0][0:1, 0:P], most_span[:, :], ident[:, :], start=True, stop=True)\
                .then_inc(r_full_dve[0], 1)
            for b in range(2):
                lo, hi = b * BLK, min((b + 1) * BLK, NT)
                take(pe, r_free[b])
                nc.tensor.matmul(ps_r[b][:, 0:hi - lo], ones[:, :], over_f[:, lo:hi], start=True, stop=True)\
                    .then_inc(r_full_dve[b], 1)
            take(pe, typ_ready)
            to_columns(f_typ)
            def take_r():
                for b in range(2):
                    take(pe, r_free[b])

            def give_r():
                for b in range(2):
                    pe.sem_inc(r_free[b], 1)

            def send_blocks(transpose):
                for n in range(NB):
                    if n >= BANKS:
                        take(pe, block_free[n % BANKS])
                    for s in blocks_of(n):
                        ins = transpose(banks[n % BANKS], s, (s - n * TB) * P, tile_rows(s))
                    ins.then_inc(block_full[n % BANKS], 1)
                for i in range(BANKS):
                    take(pe, block_free[i])

            def to_rows(bank, s, at, part):
                return nc.tensor.transpose(bank[0:part, at:at + D], out_t[:, s * P:s * P + part], ident[:, :])

            def root_block(n, b):
                take(pe, r_free[b])
                nc.tensor.matmul(ps_r[b][:, 0:block_cols(n)], w_root[:, :],
                                 h_t[:, n * BLK:n * BLK + block_cols(n)],
                                 start=True, stop=True).then_inc(r_full_act[b], 1)

            def count_units():
                for h in range(UNITS):
                    take(pe, unit_full[h])
                    for t in range(CT):
                        ins = nc.tensor.matmul(ps_c[h][0:CELLS, 0:BWIN], count_cell[:, h, :, t],
                                               count_bkt[:, h, :, t], start=(t == 0), stop=(t == CT - 1))
                    ins.then_inc(unit_free[h], 1)

            take(pe, passes_ready[0])
            count_of = load_passes(pe)
            rest = load_value(pe, passes[0:1, 3:4], NU // UNITS - (NB - 1) * PER, BUCKETS * NU,
                              "what the other blocks leave of it")[0]
            pe.wait_ge(x_in, 32)
            for n in range(NB):
                b = n % 2
                take(pe, r_free[b])
                for s in blocks_of(n):
                    part, at = tile_rows(s), (s - n * TB) * P
                    ins = nc.tensor.transpose(ps_r[b][:, at:at + part], x_rows[0:part, s, :],
                                              ident[0:part, 0:part])
                ins.then_inc(r_full_act[b], 1)
                if n == 0 or PER > 1:
                    with pe.Fori(0, rest if n == 0 else PER):
                        count_units()
                else:
                    count_units()
            take_r()
            give_r()
            take(pe, w_ready)
            for n in range(NB):
                root_block(n, n % 2)

            def turn(q, bank):
                b = q % 2
                take(pe, cell_full[b])
                for t in range(GT):
                    ins = nc.tensor.matmul(bank[0:CELLS, t * P:(t + 1) * P], oh_cell[:, b, :, t], ident_bf[:, :],
                                           start=True, stop=True)
                ins.then_inc(r_full_act[b], 1)

            def look_up(start, q):
                b = (q + G) % 2
                u = max(i for i, lo in enumerate(LOOKS) if lo <= q % G)
                r = u % 2
                bucket = load_buckets(pe, start + q * GT, GT)
                if q % G == LOOKS[u]:
                    take(pe, weights_free[r])
                take(pe, turned_full[b])
                for t in range(GT):
                    at = ((q % G - LOOKS[u]) * GT + t) * NEAR * PARTS
                    ins = nc.tensor.matmul(ps_w[r][:, at:at + NEAR * PARTS], oh_cell_t[:, b, t * P:(t + 1) * P],
                                           inv_parts[:, bass.ds(bucket[t], NEAR), :].rearrange("p w k -> p (w k)"),
                                           start=True, stop=True)
                ins.then_inc(turned_free[b], 1)
                if q % G + 1 == LOOKS[u + 1]:
                    nc.tensor.matmul(ps_w[r][:, BLK - 1:BLK], zeros[:, :], zeros[:, 0:1], start=True, stop=True)\
                        .then_inc(weights_full[r], 1)

            done_of = pe.alloc_register("gathers_done")
            pe.reg_mov(done_of, 0)

            def sum_edges(q, target):
                b = q % 2
                take(pe, oh_full[b])
                if b == 0:
                    take(pe, a_free)
                pe.wait_ge(gathered[q], target)
                for t in range(GT):
                    ins = nc.tensor.matmul(ps_a[b][:, t * KEYS:(t + 1) * KEYS], ring[:, q, t, :],
                                           onehot[:, b, t, :], start=True, stop=True)
                ins.then_inc(a_full[b], 1)

            def apply_types(u):
                b = u % 2
                take(pe, sums_full[b])
                take(pe, o_free[b])
                for r in range(R):
                    ins = nc.tensor.matmul(ps_o[b][:, 0:PAIR * WIN], w_rel[:, r, :],
                                           sums[:, b, r, :, :].rearrange("p t w -> p (t w)"),
                                           start=(r == 0), stop=(r == R - 1))
                ins.then_inc(o_full[b], 1)

            def layer_sums():
                take_r()
                with pe.Fori(0, count_of):
                    take(pe, windows_full)
                    turn(G - AHEAD, banks[0])
                    turn(G - AHEAD + 1, banks[1])
                    for q in range(-AHEAD, 0):
                        if q + 2 < 0:
                            turn(q + 2 + G, banks[(q + 2 + AHEAD) % 4])
                        look_up(AHEAD * GT, q)
                    with pe.Fori(0, NL) as it:
                        pe.reg_add(done_of, done_of, GT * 16)
                        target = pe.snap(done_of)
                        after = it * (G * GT) + AHEAD * GT
                        sum_edges(0, target)
                        for q in range(G):
                            if q + 1 < G:
                                sum_edges(q + 1, target)
                            if q % 2 == 1:
                                apply_types(q // 2)
                            if q >= 1:
                                turn(q - 1, ps_r[(q - 1) % 2])
                            if q >= 2:
                                look_up(after, q - 2)
                        turn(G - 1, ps_r[1])
                        look_up(after, G - 2)
                        look_up(after, G - 1)
                    pe.sem_inc(windows_free, 1)
                    take(pe, sums_ready[0])

            with pe.Fori(0, L - 1):
                layer_sums()
                pe.sem_inc(w_used, 1)
                send_blocks(to_rows)
                give_r()
                take(pe, w_ready)
                take(pe, h_ready)
                for n in range(NB):
                    root_block(n, n % 2)
            layer_sums()

            def with_residual(bank, s, at, part):
                nc.tensor.matmul(bank[0:part, at:at + D], out_t[:, s * P:s * P + part], ident[:, :],
                                 start=True, stop=False)
                return nc.tensor.matmul(bank[0:part, at:at + D], ident[0:part, 0:part], x_again[0:part, s, :],
                                        start=False, stop=True)

            pe.wait_ge(x_in, 64)
            send_blocks(with_residual)


_INS = ["x", "src", "dst", "edge_type_8", "L0_gnn_Ws", "L0_gnn_W_roots", "L0_gnn_bs"]


def kernel(**inputs):
    import numpy as _np
    import concourse.bacc as _bacc
    from concourse import mybir as _mybir
    from concourse.bass_utils import run_bass_kernel_spmd as _run

    nc = _bacc.Bacc("TRN2", target_bir_lowering=False, num_devices=1)
    arrays, args = {}, []
    for name in _INS:
        a = _np.ascontiguousarray(inputs[name])
        arrays[f"in_{name}"] = a
        args.append(nc.dram_tensor(f"in_{name}", a.shape, _mybir.dt.from_np(a.dtype), kind="ExternalInput").ap())
    out = nc.dram_tensor("out_rows", (N, D), F32, kind="ExternalOutput").ap()
    table = nc.dram_tensor("node_table", (N, D), F32, kind="Internal").ap()
    rgcn(nc, *args, out, table)
    r = _run(nc, [arrays], core_ids=[0])
    return r.results[0]["out_rows"]
```
